# Optimizing a Trainium2 kernel written in Bass

```python
import numpy as np
import jax
import jax.numpy as jnp

def _softmax(x, axis=-1):
    return jax.nn.softmax(x, axis=axis)

def _gelu(x):
    return jax.nn.gelu(x, approximate=True)

def _silu(x):
    return jax.nn.silu(x)

def _sigmoid(x):
    return jax.nn.sigmoid(x)

def _layernorm(x, axis=-1, eps=1e-05):
    m = jnp.mean(x, axis=axis, keepdims=True)
    v = jnp.var(x, axis=axis, keepdims=True)
    return (x - m) / jnp.sqrt(v + eps)

def _scatter_add(tgt, idx, src, axis=0):
    return tgt.at[idx].add(src)

def _segment_sum(src, seg, n):
    return jax.ops.segment_sum(src, seg, n)
kernel_name = 'mk_adj_resnorm_d1_adj_r2_8797a3'

def setup_inputs(seed: int=0):
    np.random.seed(seed)
    _w = jnp.asarray

    def _rec_inputs():
        import jax
        import jax.numpy as jnp
        _gk = jax.random.key(seed)
        x = -0.0002928 + 1 * jax.random.normal(jax.random.fold_in(_gk, 1), (8, 1024, 128), jnp.float32)
        _w = (1.0 + jnp.arange(1024, dtype=jnp.float32)) ** (-0.5)
        _w = _w / _w.mean()
        _pij = jnp.clip(0.0078125 * _w[:, None] * _w[None, :], 0.0, 1.0)
        _a = jax.random.uniform(jax.random.fold_in(_gk, 2), (8, 1024, 1024)) < _pij
        _af = _a.astype(jnp.float32)
        adj = _af
        _nm = jnp.ones((8, 1024), dtype=bool)
        nodemask = jnp.where(_nm, 1.0, 0.0).astype(jnp.float32)
        return (x, adj, nodemask)
    x, adj, nodemask = _rec_inputs()

    def _L0_gnn_setup():
        import jax, jax.numpy as jnp
        import numpy as np
        B, N, C, L = (32, 512, 128, 4)

        def _gru_cell(m, h, w_ih, w_hh, b_ih, b_hh):
            gx = m @ w_ih.T + b_ih
            gh = h @ w_hh.T + b_hh
            xr, xz, xn = jnp.split(gx, 3, axis=-1)
            hr, hz, hn = jnp.split(gh, 3, axis=-1)
            r = jax.nn.sigmoid(xr + hr)
            z = jax.nn.sigmoid(xz + hz)
            n = jnp.tanh(xn + r * hn)
            return (1.0 - z) * n + z * h
        key = jax.random.key(seed)
        ks = jax.random.split(key, 8)
        x = jax.random.normal(ks[0], (B, N, C), dtype=jnp.float32)
        adj = jax.random.randint(ks[1], (B, N, N), 0, 2).astype(jnp.float32)
        mask = jnp.ones((B, N), dtype=jnp.float32)
        s = 1.0 / np.sqrt(C)
        weight = jax.random.uniform(ks[2], (L, C, C), minval=-s, maxval=s, dtype=jnp.float32)
        w_ih = jax.random.uniform(ks[3], (L, 3 * C, C), minval=-s, maxval=s, dtype=jnp.float32)
        w_hh = jax.random.uniform(ks[4], (L, 3 * C, C), minval=-s, maxval=s, dtype=jnp.float32)
        b_ih = jax.random.uniform(ks[5], (L, 3 * C), minval=-s, maxval=s, dtype=jnp.float32)
        b_hh = jax.random.uniform(ks[6], (L, 3 * C), minval=-s, maxval=s, dtype=jnp.float32)
        return {'x': x, 'adj': adj, 'mask': mask, 'weight': weight, 'w_ih': w_ih, 'w_hh': w_hh, 'b_ih': b_ih, 'b_hh': b_hh}
    _L0_gnn_all = _L0_gnn_setup()
    _L0_gnn_in = {k: v for k, v in _L0_gnn_all.items() if k in ('weight', 'w_ih', 'w_hh', 'b_ih', 'b_hh')}
    del _L0_gnn_all
    return {'x': x, 'adj': adj, 'nodemask': nodemask, 'L0_gnn_weight': _L0_gnn_in['weight'], 'L0_gnn_w_ih': _L0_gnn_in['w_ih'], 'L0_gnn_w_hh': _L0_gnn_in['w_hh'], 'L0_gnn_b_ih': _L0_gnn_in['b_ih'], 'L0_gnn_b_hh': _L0_gnn_in['b_hh']}

def reference(x, adj, nodemask, L0_gnn_weight, L0_gnn_w_ih, L0_gnn_w_hh, L0_gnn_b_ih, L0_gnn_b_hh):
    import jax
    import jax.numpy as jnp

    def _L0_gnn_ref(x, adj, mask, weight, w_ih, w_hh, b_ih, b_hh):
        import jax, jax.numpy as jnp
        import numpy as np
        B, N, C, L = (32, 512, 128, 4)

        def _gru_cell(m, h, w_ih, w_hh, b_ih, b_hh):
            gx = m @ w_ih.T + b_ih
            gh = h @ w_hh.T + b_hh
            xr, xz, xn = jnp.split(gx, 3, axis=-1)
            hr, hz, hn = jnp.split(gh, 3, axis=-1)
            r = jax.nn.sigmoid(xr + hr)
            z = jax.nn.sigmoid(xz + hz)
            n = jnp.tanh(xn + r * hn)
            return (1.0 - z) * n + z * h
        h = x
        for i in range(L):
            hw = jnp.einsum('bnc,cd->bnd', h, weight[i])
            m = jnp.einsum('bjn,bjd->bnd', adj, hw)
            h = _gru_cell(m, h, w_ih[i], w_hh[i], b_ih[i], b_hh[i])
        return h * mask[:, :, None]
    x = _layernorm(x + _L0_gnn_ref(x, adj, nodemask, L0_gnn_weight, L0_gnn_w_ih, L0_gnn_w_hh, L0_gnn_b_ih, L0_gnn_b_hh), axis=-1)
    return x

_drawn_inputs = setup_inputs


def setup_inputs(seed=0):
    import zlib

    import numpy as np

    out = dict(_drawn_inputs(seed))
    spreads = {}
    factors = {}
    for name, (base, spread) in spreads.items():
        noise = np.random.default_rng([zlib.crc32(name.encode()), seed]).standard_normal(out[name].shape)
        drawn = base * np.exp(spread * noise) if base else spread * noise
        out[name] = jnp.asarray(drawn.astype(out[name].dtype))
    for name, factor in factors.items():
        out[name] = (out[name] * factor).astype(out[name].dtype)
    return out
```

```python
from contextlib import ExitStack

import concourse.bass as bass
from concourse import mybir

F32 = mybir.dt.float32
F32R = mybir.dt.float32r
I32 = mybir.dt.int32
ALU = mybir.AluOpType
ACT = mybir.ActivationFunctionType
AX = mybir.AxisListType

P = 128
EPS = 1e-5


def gnn_kernel(nc, x, adj, nodemask, weight, w_ih, w_hh, b_ih, b_hh, out):
    B, N, C = x.shape
    L = weight.shape[0]
    NB = N // P
    H = N // 2
    HB = NB // 2
    G = 3
    PAIRS = B // 2
    STEPS = 2 * L
    HS = 2 * STEPS
    HS_IN = HS - 4
    LOWBITS = 0xFFF

    ctx = ExitStack()
    with ctx:
        def sb(name, shape, dt=F32):
            return ctx.enter_context(nc.sbuf_tensor(name, shape, dt))

        def sem(name):
            return ctx.enter_context(nc.semaphore(name))

        adj_hi = sb("adj_hi", [P, 2, NB, N], F32R)
        adj_in = sb("adj_in", [P, NB, N])
        x_in = sb("x_in", [P, 2, NB, C])
        y = sb("y", [P, 2, NB, C])
        nat_hi = sb("nat_hi", [P, 2, NB, C], F32R)
        nat_lo = sb("nat_lo", [P, 2, NB, C], F32R)
        hT = sb("hT", [P, 2, N])
        hT_hi = sb("hT_hi", [P, 2, N], F32R)
        hT_lo = sb("hT_lo", [P, 2, N], F32R)
        S_hi = sb("S_hi", [P, 2, H], F32R)
        S_lo = sb("S_lo", [P, 2, H], F32R)
        work = sb("work", [P, 4, 2, H])
        r_sb, z_sb, t_sb, n_sb = (work[:, i] for i in range(4))
        wx_hi = sb("wx_hi", [P, L, G * C], F32R)
        wx_lo = sb("wx_lo", [P, L, G * C], F32R)
        wh_hi = sb("wh_hi", [P, L, G * C], F32R)
        wh_lo = sb("wh_lo", [P, L, G * C], F32R)
        ident = sb("ident", [P, P])
        ones = sb("ones", [P, P])
        rows = sb("rows", [P, 2, P])
        bias = sb("bias", [P, 2, L * G])
        bsum = sb("bsum", [P, L * G])
        mask = sb("mask", [P, B * NB])
        low = sb("low", [P, N], I32)
        lowf = sb("lowf", [P, 1])
        flag = sb("flag", [P, 1], I32)
        stats = sb("stats", [P, NB, 6])
        mv = sb("mv", [P, NB, 2])
        vare = sb("vare", [P, NB])
        mhalf = sb("mhalf", [P, NB])
        rstd = sb("rstd", [P, NB])

        p_S = [ctx.enter_context(nc.psum_tensor(f"p_S{h}", [P, H], F32)) for h in range(2)]
        p_r = ctx.enter_context(nc.psum_tensor("p_r", [P, H], F32))
        p_z = ctx.enter_context(nc.psum_tensor("p_z", [P, H], F32))
        p_hn = ctx.enter_context(nc.psum_tensor("p_hn", [P, H], F32))
        p_xn = ctx.enter_context(nc.psum_tensor("p_xn", [P, H], F32))
        p_tr = [ctx.enter_context(nc.psum_tensor(f"p_tr{h}", [P, HB, P], F32)) for h in range(2)]
        p_start = [[p_S[0], p_S[1], p_r, p_z], [p_hn, p_xn, p_tr[0], p_tr[1]]]

        def flat(t):
            return t[:, :] if len(t.shape) == 2 else t[:, :, :].rearrange("p a b -> p (a b)")

        w_nat = work[:, 0].rearrange("p a b -> p (a b)")[:, 0:L * C].rearrange("p (l d) -> p l d", l=L)
        wih_nat = work[:, 1:3].rearrange("p a b c -> p (a b c)")[:, 0:L * G * C].rearrange("p (q d) -> p q d", q=L * G)
        whh_nat = hT[:, :, :].rearrange("p a b -> p (a b)")[:, 0:L * G * C].rearrange("p (q d) -> p q d", q=L * G)
        wT = y[:, 0].rearrange("p a b -> p (a b)")[:, 0:L * C]
        wihT = y[:, 1].rearrange("p a b -> p (a b)")[:, 0:2 * G * C]

        ident_zero = sem("ident_zero")
        ident_made = sem("ident_made")
        rows_in = sem("rows_in")
        w_in = sem("w_in")
        start_tr = sem("start_tr")
        start_copied = sem("start_copied")
        start_joined = sem("start_joined")
        start_hi = sem("start_hi")
        start_lo = sem("start_lo")
        rows_tr = sem("rows_tr")
        rows_out = sem("rows_out")
        adj_loaded = [sem(f"adj_loaded{j}") for j in range(NB)]
        adj_ready = sem("adj_ready")
        adj_checked = sem("adj_checked")
        low_zero = sem("low_zero")
        x_loaded = [sem(f"x_loaded{s}") for s in range(2)]
        y_loaded = [sem(f"y_loaded{s}") for s in range(2)]
        out_stored = [sem(f"out_stored{s}") for s in range(2)]
        xnat_hi = sem("xnat_hi")
        xnat_lo = sem("xnat_lo")
        x_tr = sem("x_tr")
        xT_hi = sem("xT_hi")
        xT_done = sem("xT_done")
        s_done = sem("s_done")
        s_hi_made = sem("s_hi_made")
        s_split = sem("s_split")
        hn_done = sem("hn_done")
        r_done = sem("r_done")
        xn_done = sem("xn_done")
        z_done = sem("z_done")
        r_act = sem("r_act")
        z_act = sem("z_act")
        t_mul = sem("t_mul")
        t_add = sem("t_add")
        n_act = sem("n_act")
        d_sub = sem("d_sub")
        d_mul = sem("d_mul")
        h_new = sem("h_new")
        h_hi_made = sem("h_hi_made")
        h_split = sem("h_split")
        h_tr = sem("h_tr")
        nat_hi_made = sem("nat_hi_made")
        nat_split = sem("nat_split")
        y_added = sem("y_added")
        y_stats = sem("y_stats")
        y_aggr = sem("y_aggr")
        var_eps = sem("var_eps")
        rstd_made = sem("rstd_made")
        y_normed = sem("y_normed")
        low_masked = sem("low_masked")
        low_red = sem("low_red")
        low_sum = sem("low_sum")
        flag_made = sem("flag_made")

        g_loaded = sem("g_loaded")
        g_xtr = sem("g_xtr")
        g_xT = sem("g_xT")
        g_s = sem("g_s")
        g_s_out = sem("g_s_out")
        g_gates = sem("g_gates")
        g_rz = sem("g_rz")
        g_n = sem("g_n")
        g_dve = sem("g_dve")
        g_tr = sem("g_tr")
        g_nat = sem("g_nat")
        g_added = sem("g_added")
        g_stats = sem("g_stats")
        g_aggr = sem("g_aggr")
        g_var = sem("g_var")
        g_rstd = sem("g_rstd")
        g_normed = sem("g_normed")
        CHAIN = 5
        g_S = x_in[:, 1].rearrange("p a b -> p (a b)")

        adj_v = adj.rearrange("b (j p) n -> b j p n", p=P)
        x_v = x.rearrange("b (j p) c -> b p j c", p=P)
        out_v = out.rearrange("b (j p) c -> b p j c", p=P)

        def pairs(eng, body):
            body(0, True, False)
            with eng.Fori(1, PAIRS - 1) as p:
                body(p, False, False)
            body(PAIRS - 1, False, True)

        def general(eng, body, stores=False):
            eng.wait_ge(flag_made, 1)
            with eng.If(eng.value_load(flag[0:1, 0:1], min_val=0, max_val=1) != 0):
                with eng.Fori(0, B) as b:
                    body(b)
                if stores:
                    eng.wait_ge(out_stored[1], 16 * (PAIRS + B))

        def half(h):
            return slice(h * H, (h + 1) * H)

        block = ctx.enter_context(nc.Block())

        @block.sync
        def _(sp):
            sp.dma_start(w_nat, weight.rearrange("l p d -> p l d")).then_inc(w_in, 16)
            sp.dma_start(wih_nat, w_ih.rearrange("l (q p) d -> p (l q) d", p=P)).then_inc(w_in, 16)
            sp.dma_start(whh_nat, w_hh.rearrange("l (q p) d -> p (l q) d", p=P)).then_inc(w_in, 16)
            sp.dma_start(rows[0:L * G, 0, :], b_ih.rearrange("l (q p) -> (l q) p", p=P)).then_inc(rows_in, 16)
            sp.dma_start(rows[L * G:2 * L * G, 0, :], b_hh.rearrange("l (q p) -> (l q) p", p=P)).then_inc(rows_in, 16)
            sp.dma_start(rows[0:B * NB, 1, :], nodemask.rearrange("b (j p) -> (b j) p", p=P)).then_inc(rows_in, 16)
            sp.dma_start(x_in[:, 0], x_v[0]).then_inc(x_loaded[0], 16)
            for j in range(NB):
                sp.dma_start(adj_in[:, j], adj_v[0, j]).then_inc(adj_loaded[j], 16)
            sp.dma_start(x_in[:, 1], x_v[1]).then_inc(x_loaded[1], 16)
            for j in range(NB):
                sp.wait_ge(adj_ready, j + 1)
                sp.wait_ge(adj_checked, j + 1)
                sp.dma_start(adj_in[:, j], adj_v[1, j]).then_inc(adj_loaded[j], 16)

            def next_adj(p, s):
                for j in range(NB):
                    sp.wait_ge(adj_checked, NB * (2 * p + 1 + s) + j + 1)
                    sp.wait_ge(adj_ready, NB * (2 * p + 1 + s) + j + 1)
                    sp.dma_start(adj_in[:, j], adj_v[2 * p + 2 + s, j]).then_inc(adj_loaded[j], 16)

            def store(p, s):
                sp.wait_ge(y_normed, 2 * p + s + 1)
                sp.dma_start(out_v[2 * p + s], y[:, s]).then_inc(out_stored[s], 16)

            def body(p, first, last):
                if first:
                    sp.wait_ge(start_joined, L)
                else:
                    store(p - 1, 1)
                for s in range(2):
                    if not first:
                        sp.wait_ge(out_stored[s], 16 * p)
                    sp.dma_start(y[:, s], x_v[2 * p + s]).then_inc(y_loaded[s], 16)
                if not last:
                    next_adj(p, 0)
                    for s in range(2):
                        sp.wait_ge(x_tr, 4 * p + 2 * s + 2)
                        sp.wait_ge(xnat_lo, 2 * p + s + 1)
                        sp.dma_start(x_in[:, s], x_v[2 * p + 2 + s]).then_inc(x_loaded[s], 16)
                    next_adj(p, 1)
                store(p, 0)

            pairs(sp, body)
            store(PAIRS - 1, 1)
            for s in range(2):
                sp.wait_ge(out_stored[s], 16 * PAIRS)

            def graph(b):
                sp.dma_start(adj_in[:, :, :], adj_v[b].rearrange("j p n -> p j n")).then_inc(g_loaded, 16)
                sp.dma_start(x_in[:, 0], x_v[b]).then_inc(g_loaded, 16)
                sp.wait_ge(out_stored[1], 16 * PAIRS + 16 * b)
                sp.dma_start(y[:, 0], x_v[b]).then_inc(g_loaded, 16)
                sp.wait_ge(g_normed, b + 1)
                sp.dma_start(out_v[b], y[:, 0]).then_inc(out_stored[1], 16)

            general(sp, graph, stores=True)

        @block.tensor
        def _(pe):
            pe.wait_ge(ident_made, 1)
            pe.wait_ge(w_in, 48)
            for l in range(L):
                pw, pi, ph, pj = p_start[l % 2]
                if l >= 2:
                    pe.wait_ge(start_lo, l - 1)
                nc.tensor.transpose(flat(pw)[:, 0:C], w_nat[:, l], ident[:, :])
                for q in range(G):
                    nc.tensor.transpose(flat(pi)[:, q * C:(q + 1) * C], wih_nat[:, G * l + q], ident[:, :])
                for q in range(G):
                    last = nc.tensor.transpose(flat(ph)[:, q * C:(q + 1) * C], whh_nat[:, G * l + q], ident[:, :])
                last.then_inc(start_tr, 1)
                pe.wait_ge(start_copied, l + 1)
                nc.tensor.matmul(flat(pj)[:, 0:G * C], wT[:, l * C:(l + 1) * C],
                                 wihT[:, (l % 2) * G * C:(l % 2 + 1) * G * C],
                                 start=True, stop=True).then_inc(start_joined, 1)
            pe.wait_ge(start_lo, L)
            pe.wait_ge(rows_in, 48)
            nc.tensor.transpose(p_r[:, 0:2 * L * G], rows[0:2 * L * G, 0, :], ident[0:2 * L * G, 0:2 * L * G])
            nc.tensor.transpose(p_z[:, 0:B * NB], rows[0:B * NB, 1, :], ident[0:B * NB, 0:B * NB]).then_inc(rows_tr, 1)
            pe.wait_ge(rows_out, 2)

            def transpose_x(p, s, first):
                pe.wait_ge(x_loaded[s], 16 * (p + 1))
                for h in range(2):
                    if not first:
                        pe.wait_ge(y_added, 4 * (p - 1) + 2 * s + h + 1)
                    elif s == 1:
                        pe.wait_ge(xT_done, h + 1)
                    for i in range(HB):
                        last = nc.tensor.transpose(p_tr[h][:, i, :], x_in[:, s, h * HB + i], ident[:, :])
                    last.then_inc(x_tr, 1)

            def transpose_h(p, g, h):
                pe.wait_ge(h_new, HS * p + 2 * g + h + 1)
                if g == STEPS - 1:
                    pass
                for i in range(HB):
                    n0 = h * H + i * P
                    last = nc.tensor.transpose(p_tr[h][:, i, :], hT[:, g % 2, n0:n0 + P], ident[:, :])
                last.then_inc(h_tr, 1)

            def aggregate(p, g):
                l, s = divmod(g, 2)
                if l == 0:
                    pe.wait_ge(xnat_lo, 2 * p + s + 1)
                else:
                    pe.wait_ge(nat_split, HS_IN * p + 2 * (g - 2) + 2)
                for h in range(2):
                    for j in range(NB):
                        if l == 0 and h == 0:
                            pe.wait_ge(adj_ready, NB * (2 * p + s) + j + 1)
                        for part in (nat_hi, nat_lo):
                            last = nc.tensor.matmul(p_S[h][:, :], part[:, s, j], adj_hi[:, s, j, half(h)],
                                                    start=(j == 0 and part is nat_hi),
                                                    stop=(j == NB - 1 and part is nat_lo))
                    last.then_inc(s_done, 1)

            def product(bank, w, l, q, v, start, stop):
                w_h, w_l = w
                v_h, v_l = v
                cols = slice(q * C, (q + 1) * C)
                nc.tensor.matmul(bank[:, :], w_h[:, l, cols], v_h, start=start, stop=False)
                nc.tensor.matmul(bank[:, :], w_h[:, l, cols], v_l, start=False, stop=False)
                return nc.tensor.matmul(bank[:, :], w_l[:, l, cols], v_h, start=False, stop=stop)

            def gates(p, g, h, first):
                l, s = divmod(g, 2)
                k = 2 * g + h
                if l == 0:
                    pe.wait_ge(xT_done, 4 * p + k + 1)
                else:
                    pe.wait_ge(h_split, HS_IN * p + k - 4 + 1)
                state = (hT_hi[:, s, half(h)], hT_lo[:, s, half(h)])
                fed = (S_hi[:, h], S_lo[:, h])
                prior = not (first and k == 0)
                if prior:
                    pe.wait_ge(r_act, HS * p + k)
                product(p_r, (wh_hi, wh_lo), l, 0, state, True, False)
                if prior:
                    pe.wait_ge(z_act, HS * p + k)
                product(p_z, (wh_hi, wh_lo), l, 1, state, True, False)
                if prior:
                    pe.wait_ge(t_mul, HS * p + k)
                product(p_hn, (wh_hi, wh_lo), l, 2, state, True, True).then_inc(hn_done, 1)
                pe.wait_ge(s_split, HS * p + k + 1)
                product(p_r, (wx_hi, wx_lo), l, 0, fed, False, True).then_inc(r_done, 1)
                if prior:
                    pe.wait_ge(t_add, HS * p + k)
                product(p_xn, (wx_hi, wx_lo), l, 2, fed, True, True).then_inc(xn_done, 1)
                product(p_z, (wx_hi, wx_lo), l, 1, fed, False, True).then_inc(z_done, 1)

            def transpose_former(p, g, h, first):
                if g == 0:
                    if not first:
                        pe.wait_ge(xT_done, 4 * p + h + 1)
                        transpose_h(p - 1, STEPS - 1, h)
                else:
                    if g == 1:
                        pe.wait_ge(xT_done, 4 * p + 2 + h + 1)
                    else:
                        pe.wait_ge(nat_split, HS_IN * p + 2 * (g - 2) + h + 1)
                    transpose_h(p, g - 1, h)

            def body(p, first, last):
                for g in range(STEPS):
                    if g < 2:
                        transpose_x(p, g, first)
                    aggregate(p, g)
                    for h in range(2):
                        transpose_former(p, g, h, first)
                        gates(p, g, h, first)

            pairs(pe, body)
            for h in range(2):
                pe.wait_ge(y_added, 4 * (PAIRS - 1) + h + 1)
                transpose_h(PAIRS - 1, STEPS - 1, h)
            pe.wait_ge(low_red, 1)
            nc.tensor.matmul(p_r[:, 0:1], ones[:, :], lowf[:, 0:1], start=True, stop=True).then_inc(low_sum, 1)

            def graph(b):
                pe.wait_ge(g_loaded, 48 * b + 48)
                for h in range(2):
                    for i in range(HB):
                        last = nc.tensor.transpose(p_tr[h][:, i, :], x_in[:, 0, h * HB + i], ident[:, :])
                    last.then_inc(g_xtr, 1)
                for l in range(L):
                    if l:
                        pe.wait_ge(g_nat, (L - 1) * b + l)
                    for h in range(2):
                        for j in range(NB):
                            last = nc.tensor.matmul(p_S[h][:, :], x_in[:, 0, j], adj_in[:, j, half(h)],
                                                    start=(j == 0), stop=(j == NB - 1))
                        last.then_inc(g_s, 1)
                    for h in range(2):
                        m = 2 * L * b + 2 * l + h
                        if l == 0:
                            pe.wait_ge(g_xT, 2 * b + h + 1)
                        if l or h:
                            pe.wait_ge(g_dve, CHAIN * m)
                        pe.wait_ge(g_s_out, m + 1)
                        for bank, q, fed, state in ((p_r, 0, True, True), (p_z, 1, True, True),
                                                    (p_hn, 2, False, True), (p_xn, 2, True, False)):
                            terms = []
                            if fed:
                                terms += [(w, g_S[:, half(h)]) for w in (wx_hi, wx_lo)]
                            if state:
                                terms += [(w, hT[:, 0, half(h)]) for w in (wh_hi, wh_lo)]
                            for n, (w, v) in enumerate(terms):
                                last = nc.tensor.matmul(bank[:, :], w[:, l, q * C:(q + 1) * C].bitcast(F32), v,
                                                        start=(n == 0), stop=(n == len(terms) - 1))
                        last.then_inc(g_gates, 1)
                    pe.wait_ge(g_dve, CHAIN * (2 * L * b + 2 * l + 2))
                    for j in range(NB):
                        last = nc.tensor.transpose(p_tr[j // HB][:, j % HB, :], hT[:, 0, j * P:(j + 1) * P], ident[:, :])
                    last.then_inc(g_tr, 1)

            general(pe, graph)

        @block.scalar
        def _(act):
            def copy(dst, src):
                return nc.scalar.activation(dst, src, ACT.Copy)

            for l in range(L):
                pw, pi, ph, pj = p_start[l % 2]
                act.wait_ge(start_tr, l + 1)
                copy(wh_hi[:, l], flat(ph)[:, 0:G * C])
                act.wait_ge(start_joined, l + 1)
                copy(wx_hi[:, l], flat(pj)[:, 0:G * C]).then_inc(start_hi, 1)

            def take_adj(p, s, j):
                act.wait_ge(adj_loaded[j], 16 * (2 * p + s + 1))
                copy(adj_hi[:, s, j], adj_in[:, j]).then_inc(adj_ready, 1)

            def split_x(p, s, first):
                act.wait_ge(x_loaded[s], 16 * (p + 1))
                if not first:
                    act.wait_ge(s_done, HS * (p - 1) + 2 * (STEPS - 2 + s) + 2)
                copy(nat_hi[:, s], x_in[:, s]).then_inc(xnat_hi, 1)

            def take_xT(p, s):
                for h in range(2):
                    act.wait_ge(x_tr, 4 * p + 2 * s + h + 1)
                    copy(hT[:, s, half(h)], flat(p_tr[h]))
                    copy(hT_hi[:, s, half(h)], flat(p_tr[h])).then_inc(xT_hi, 1)

            def take_former(p, g, h):
                act.wait_ge(h_tr, HS * p + 2 * g + h + 1)
                copy(nat_hi[:, g % 2, h * HB:(h + 1) * HB], p_tr[h][:, :, :]).then_inc(nat_hi_made, 1)

            def body(p, first, last):
                for g in range(STEPS):
                    l, s = divmod(g, 2)
                    if l == 0:
                        take_xT(p, s)
                    for h in range(2):
                        act.wait_ge(s_done, HS * p + 2 * g + h + 1)
                        copy(S_hi[:, h], p_S[h][:, :]).then_inc(s_hi_made, 1)
                    if g == STEPS - 1 and not last:
                        split_x(p + 1, 0, False)
                    for h in range(2):
                        k = 2 * g + h
                        if 1 <= g <= STEPS - 2:
                            take_former(p, g - 1, h)
                        act.wait_ge(r_done, HS * p + k + 1)
                        nc.scalar.activation(r_sb[:, h], p_r[:, :], ACT.Sigmoid,
                                             bias=bsum[:, G * l:G * l + 1]).then_inc(r_act, 1)
                        act.wait_ge(z_done, HS * p + k + 1)
                        nc.scalar.activation(z_sb[:, h], p_z[:, :], ACT.Sigmoid,
                                             bias=bsum[:, G * l + 1:G * l + 2]).then_inc(z_act, 1)
                        act.wait_ge(t_add, HS * p + k + 1)
                        nc.scalar.activation(n_sb[:, h], t_sb[:, h], ACT.Tanh,
                                             bias=bias[:, 0, G * l + 2:G * l + 3]).then_inc(n_act, 1)
                        if l < L - 1:
                            act.wait_ge(h_new, HS * p + k + 1)
                            copy(hT_hi[:, s, half(h)], hT[:, s, half(h)]).then_inc(h_hi_made, 1)
                        if g == 0:
                            if h == 0 and not first:
                                act.wait_ge(s_done, HS * (p - 1) + 2 * (STEPS - 1) + 2)
                            for j in range(h * HB, (h + 1) * HB):
                                take_adj(p, 1, j)
                        elif g == STEPS - 1 and not last:
                            for j in range(h * HB, (h + 1) * HB):
                                take_adj(p + 1, 0, j)
                    if g == 0:
                        split_x(p, 1, first)

            split_x(0, 0, True)
            for j in range(NB):
                take_adj(0, 0, j)
            act.wait_ge(rows_out, 2)
            pairs(act, body)

            def graph(b):
                for h in range(2):
                    act.wait_ge(g_xtr, 2 * b + h + 1)
                    copy(hT[:, 0, half(h)], flat(p_tr[h])).then_inc(g_xT, 1)
                for l in range(L):
                    for h in range(2):
                        act.wait_ge(g_s, 2 * L * b + 2 * l + h + 1)
                        copy(g_S[:, half(h)], p_S[h][:, :]).then_inc(g_s_out, 1)
                    for h in range(2):
                        m = 2 * L * b + 2 * l + h
                        act.wait_ge(g_gates, m + 1)
                        nc.scalar.activation(r_sb[:, 0], p_r[:, :], ACT.Sigmoid, bias=bsum[:, G * l:G * l + 1])
                        nc.scalar.activation(z_sb[:, 0], p_z[:, :], ACT.Sigmoid,
                                             bias=bsum[:, G * l + 1:G * l + 2]).then_inc(g_rz, 1)
                        act.wait_ge(g_dve, CHAIN * m + 2)
                        nc.scalar.activation(n_sb[:, 0], t_sb[:, 0], ACT.Tanh,
                                             bias=bias[:, 0, G * l + 2:G * l + 3]).then_inc(g_n, 1)

            general(act, graph)

        @block.vector
        def _(dve):
            def lo(dst, src, hi):
                return nc.vector.tensor_tensor(dst, src, hi.bitcast(F32), ALU.subtract)

            nc.vector.memset(ones[:, :], 1.0)
            nc.vector.memset(low[:, :], 0).then_inc(low_zero, 1)
            dve.wait_ge(low_zero, 1)
            for l in range(L):
                pw, pi, ph, pj = p_start[l % 2]
                dve.wait_ge(start_tr, l + 1)
                if l >= 2:
                    dve.wait_ge(start_joined, l - 1)
                nc.vector.tensor_copy(wT[:, l * C:(l + 1) * C], flat(pw)[:, 0:C])
                nc.vector.tensor_copy(wihT[:, (l % 2) * G * C:(l % 2 + 1) * G * C],
                                      flat(pi)[:, 0:G * C]).then_inc(start_copied, 1)
                dve.wait_ge(start_hi, l + 1)
                lo(wh_lo[:, l], flat(ph)[:, 0:G * C], wh_hi[:, l])
                lo(wx_lo[:, l], flat(pj)[:, 0:G * C], wx_hi[:, l]).then_inc(start_lo, 1)
            dve.wait_ge(rows_tr, 1)
            nc.vector.tensor_copy(bias[:, :, :].rearrange("p a b -> p (a b)"), p_r[:, 0:2 * L * G]).then_inc(rows_out, 1)
            nc.vector.tensor_copy(mask[:, :], p_z[:, 0:B * NB])
            dve.wait_ge(rows_out, 1)
            nc.vector.tensor_tensor(bsum[:, :], bias[:, 0], bias[:, 1], ALU.add).then_inc(rows_out, 1)

            def check_adj(p, s, j, first=False):
                dve.wait_ge(adj_loaded[j], 16 * (2 * p + s + 1))
                if not (first and s == 0 and j == 0):
                    dve.wait_ge(adj_checked, NB * (2 * p + s) + j)
                nc.vector.tensor_tensor(low[:, :], low[:, :], adj_in[:, j].bitcast(I32),
                                        ALU.bitwise_or).then_inc(adj_checked, 1)

            def split_x(p, s):
                dve.wait_ge(xnat_hi, 2 * p + s + 1)
                lo(nat_lo[:, s], x_in[:, s], nat_hi[:, s]).then_inc(xnat_lo, 1)

            def take_xT(p, s):
                for h in range(2):
                    dve.wait_ge(xT_hi, 4 * p + 2 * s + h + 1)
                    lo(hT_lo[:, s, half(h)], flat(p_tr[h]), hT_hi[:, s, half(h)]).then_inc(xT_done, 1)

            def take_former(p, g, h):
                dve.wait_ge(nat_hi_made, HS_IN * p + 2 * g + h + 1)
                lo(nat_lo[:, g % 2, h * HB:(h + 1) * HB], p_tr[h][:, :, :],
                   nat_hi[:, g % 2, h * HB:(h + 1) * HB]).then_inc(nat_split, 1)

            def residual(p, s, h):
                if h == 0:
                    dve.wait_ge(y_loaded[s], 16 * (p + 1))
                dve.wait_ge(h_tr, HS * p + 2 * (STEPS - 2 + s) + h + 1)
                for i in range(HB):
                    j = h * HB + i
                    col = NB * (2 * p + s) + j
                    last = nc.vector.scalar_tensor_tensor(y[:, s, j], p_tr[h][:, i, :], mask[:, bass.ds(col, 1)],
                                                          y[:, s, j], ALU.mult, ALU.add)
                last.then_inc(y_added, 1)
                dve.wait_ge(y_added, 4 * p + 2 * s + h + 1)
                for i in range(HB):
                    j = h * HB + i
                    last = nc.vector.bn_stats(stats[:, j], y[:, s, j])
                last.then_inc(y_stats, 1)

            def wait_stats(p, s, h):
                dve.wait_ge(y_stats, 4 * p + 2 * s + h + 1)

            def moments(s, h):
                for j in range(h * HB, (h + 1) * HB):
                    last = nc.vector.bn_aggr(mv[:, j], stats[:, j])
                if h == 1:
                    last.then_inc(y_aggr, 1)

            def variance_eps(p, s):
                dve.wait_ge(y_aggr, 2 * p + s + 1)
                nc.vector.tensor_scalar(vare[:, :], mv[:, :, 1], EPS, None, ALU.add).then_inc(var_eps, 1)

            def normalise(p, s):
                dve.wait_ge(rstd_made, 2 * p + s + 1)
                for j in range(NB):
                    last = nc.vector.tensor_scalar(y[:, s, j], y[:, s, j], mv[:, j, 0:1], rstd[:, j:j + 1],
                                                   ALU.subtract, ALU.mult)
                last.then_inc(y_normed, 1)

            def body(p, first, last):
                for g in range(STEPS):
                    l, s = divmod(g, 2)
                    if l == 0:
                        take_xT(p, s)
                    for h in range(2):
                        dve.wait_ge(s_hi_made, HS * p + 2 * g + h + 1)
                        lo(S_lo[:, h], p_S[h][:, :], S_hi[:, h]).then_inc(s_split, 1)
                    if g == STEPS - 1 and not last:
                        split_x(p + 1, 0)
                    for h in range(2):
                        k = 2 * g + h
                        finishing = None
                        if 1 <= g <= STEPS - 2:
                            take_former(p, g - 1, h)
                        elif g == STEPS - 1:
                            finishing = (p, 0)
                        elif not first:
                            finishing = (p - 1, 1)
                        if finishing:
                            residual(*finishing, h)
                            wait_stats(*finishing, h)
                        dve.wait_ge(hn_done, HS * p + k + 1)
                        dve.wait_ge(r_act, HS * p + k + 1)
                        nc.vector.scalar_tensor_tensor(t_sb[:, h], p_hn[:, :], bias[:, 1, G * l + 2:G * l + 3],
                                                       r_sb[:, h], ALU.add, ALU.mult).then_inc(t_mul, 1)
                        if finishing:
                            moments(finishing[1], h)
                        dve.wait_ge(xn_done, HS * p + k + 1)
                        dve.wait_ge(t_mul, HS * p + k + 1)
                        nc.vector.tensor_tensor(t_sb[:, h], p_xn[:, :], t_sb[:, h], ALU.add).then_inc(t_add, 1)
                        if g == 0:
                            for j in range(h * HB, (h + 1) * HB):
                                check_adj(p, 1, j)
                        elif g in (2, 3) and not last:
                            for j in range(HB * (g - 2) + 2 * h, HB * (g - 2) + 2 * h + 2):
                                check_adj(p + 1, 0, j)
                        if finishing and h == 1:
                            variance_eps(*finishing)
                        dve.wait_ge(d_mul, HS * p + k + 1)
                        nc.vector.tensor_tensor(hT[:, s, half(h)], n_sb[:, h], t_sb[:, h], ALU.add).then_inc(h_new, 1)
                        if finishing and h == 1:
                            normalise(*finishing)
                        if l < L - 1:
                            dve.wait_ge(h_hi_made, HS_IN * p + k + 1)
                            lo(hT_lo[:, s, half(h)], hT[:, s, half(h)], hT_hi[:, s, half(h)]).then_inc(h_split, 1)
                    if g == 0:
                        split_x(p, 1)

            split_x(0, 0)
            for j in range(NB):
                check_adj(0, 0, j, True)
            pairs(dve, body)
            for h in range(2):
                residual(PAIRS - 1, 1, h)
                wait_stats(PAIRS - 1, 1, h)
                moments(1, h)
            variance_eps(PAIRS - 1, 1)
            normalise(PAIRS - 1, 1)

            dve.wait_ge(adj_checked, B * NB)
            nc.vector.tensor_scalar(low[:, :], low[:, :], LOWBITS, None, ALU.bitwise_and).then_inc(low_masked, 1)
            dve.wait_ge(low_masked, 1)
            nc.vector.tensor_reduce(lowf[:, :], low[:, :], AX.X, ALU.max).then_inc(low_red, 1)
            dve.wait_ge(low_sum, 1)
            nc.vector.tensor_scalar(flag[:, :], p_r[:, 0:1], 0.0, None, ALU.is_gt).then_inc(flag_made, 1)

            def graph(b):
                for l in range(L):
                    for h in range(2):
                        m = 2 * L * b + 2 * l + h
                        n, t, z = n_sb[:, 0], t_sb[:, 0], z_sb[:, 0]
                        dve.wait_ge(g_rz, m + 1)
                        nc.vector.scalar_tensor_tensor(t, p_hn[:, :], bias[:, 1, G * l + 2:G * l + 3],
                                                       r_sb[:, 0], ALU.add, ALU.mult).then_inc(g_dve, 1)
                        dve.wait_ge(g_dve, CHAIN * m + 1)
                        nc.vector.tensor_tensor(t, p_xn[:, :], t, ALU.add).then_inc(g_dve, 1)
                        dve.wait_ge(g_n, m + 1)
                        nc.vector.tensor_tensor(t, hT[:, 0, half(h)], n, ALU.subtract).then_inc(g_dve, 1)
                        dve.wait_ge(g_dve, CHAIN * m + 3)
                        nc.vector.tensor_tensor(t, z, t, ALU.mult).then_inc(g_dve, 1)
                        dve.wait_ge(g_dve, CHAIN * m + 4)
                        nc.vector.tensor_tensor(hT[:, 0, half(h)], n, t, ALU.add).then_inc(g_dve, 1)
                    dve.wait_ge(g_tr, L * b + l + 1)
                    for h in range(2):
                        if l < L - 1:
                            last = nc.vector.tensor_copy(x_in[:, 0, h * HB:(h + 1) * HB], p_tr[h][:, :, :])
                        if l == L - 1:
                            for i in range(HB):
                                j = h * HB + i
                                last = nc.vector.scalar_tensor_tensor(
                                    y[:, 0, j], p_tr[h][:, i, :], mask[:, bass.ds(NB * b + j, 1)], y[:, 0, j],
                                    ALU.mult, ALU.add)
                    last.then_inc(g_nat if l < L - 1 else g_added, 1)
                dve.wait_ge(g_added, b + 1)
                for j in range(NB):
                    last = nc.vector.bn_stats(stats[:, j], y[:, 0, j])
                last.then_inc(g_stats, 1)
                dve.wait_ge(ident_made, 1)
                dve.wait_ge(g_stats, b + 1)
                for j in range(NB):
                    last = nc.vector.bn_aggr(mv[:, j], stats[:, j])
                last.then_inc(g_aggr, 1)
                dve.wait_ge(g_aggr, b + 1)
                nc.vector.tensor_scalar(vare[:, :], mv[:, :, 1], EPS, None, ALU.add).then_inc(g_var, 1)
                dve.wait_ge(g_rstd, b + 1)
                for j in range(NB):
                    last = nc.vector.tensor_scalar(y[:, 0, j], y[:, 0, j], mv[:, j, 0:1], rstd[:, j:j + 1],
                                                   ALU.subtract, ALU.mult)
                last.then_inc(g_normed, 1)

            general(dve, graph)

        @block.gpsimd
        def _(pool):
            nc.gpsimd.memset(ident[:, :], 0.0).then_inc(ident_zero, 1)
            pool.wait_ge(ident_zero, 1)
            nc.gpsimd.affine_select(out=ident[:, :], in_=ident[:, :], compare_op=ALU.not_equal, fill=1.0,
                                    base=0, pattern=[[-1, P]], channel_multiplier=1).then_inc(ident_made, 1)
            nc.gpsimd.memset(mhalf[:, :], -0.5)

            def inverse_deviation(p, s):
                pool.wait_ge(var_eps, 2 * p + s + 1)
                nc.gpsimd.tensor_tensor(rstd[:, :], vare[:, :], mhalf[:, :], ALU.pow).then_inc(rstd_made, 1)

            def body(p, first, last):
                for g in range(STEPS):
                    l, s = divmod(g, 2)
                    for h in range(2):
                        k = 2 * g + h
                        if h == 1 and g == 0 and not first:
                            inverse_deviation(p - 1, 1)
                        if h == 1 and g == STEPS - 1:
                            inverse_deviation(p, 0)
                        pool.wait_ge(n_act, HS * p + k + 1)
                        nc.gpsimd.tensor_tensor(t_sb[:, h], hT[:, s, half(h)], n_sb[:, h],
                                                ALU.subtract).then_inc(d_sub, 1)
                        pool.wait_ge(d_sub, HS * p + k + 1)
                        nc.gpsimd.tensor_tensor(t_sb[:, h], z_sb[:, h], t_sb[:, h],
                                                ALU.mult).then_inc(d_mul, 1)

            pairs(pool, body)
            inverse_deviation(PAIRS - 1, 1)

            def graph(b):
                pool.wait_ge(g_var, b + 1)
                nc.gpsimd.tensor_tensor(rstd[:, :], vare[:, :], mhalf[:, :], ALU.pow).then_inc(g_rstd, 1)

            general(pool, graph)


_INS = ['x', 'adj', 'nodemask', 'L0_gnn_weight', 'L0_gnn_w_ih', 'L0_gnn_w_hh', 'L0_gnn_b_ih', 'L0_gnn_b_hh']


def kernel(**inputs):
    import numpy as _np
    import concourse.bacc as _bacc
    from concourse import mybir as _mybir
    from concourse.bass_utils import run_bass_kernel_spmd as _run

    nc = _bacc.Bacc("TRN2", target_bir_lowering=False, num_devices=1)
    arrays, args = {}, []
    for name in _INS:
        a = _np.ascontiguousarray(inputs[name])
        arrays[f"in_{name}_dram"] = a
        args.append(nc.dram_tensor(f"in_{name}_dram", a.shape, _mybir.dt.from_np(a.dtype), kind="ExternalInput").ap())
    out = nc.dram_tensor("out_0_dram", inputs["x"].shape, _mybir.dt.float32, kind="ExternalOutput").ap()
    gnn_kernel(nc, *args, out)
    r = _run(nc, [arrays], core_ids=[0])
    return r.results[0]["out_0_dram"]
```

```python
from contextlib import ExitStack

import concourse.bass as bass
from concourse import mybir

F32 = mybir.dt.float32
F32R = mybir.dt.float32r
I32 = mybir.dt.int32
ALU = mybir.AluOpType
ACT = mybir.ActivationFunctionType
AX = mybir.AxisListType

P = 128
EPS = 1e-5


def gnn_kernel(nc, x, adj, nodemask, weight, w_ih, w_hh, b_ih, b_hh, out):
    B, N, C = x.shape
    L = weight.shape[0]
    NB = N // P
    H = N // 2
    HB = NB // 2
    G = 3
    PAIRS = B // 2
    STEPS = 2 * L
    HS = 2 * STEPS
    HS_IN = HS - 4
    LOWBITS = 0xFFF

    ctx = ExitStack()
    with ctx:
        def sb(name, shape, dt=F32):
            return ctx.enter_context(nc.sbuf_tensor(name, shape, dt))

        def sem(name):
            return ctx.enter_context(nc.semaphore(name))

        adj_hi = sb("adj_hi", [P, 2, NB, N], F32R)
        adj_in = sb("adj_in", [P, NB, N])
        x_in = sb("x_in", [P, 2, NB, C])
        y = sb("y", [P, 2, NB, C])
        nat_hi = sb("nat_hi", [P, 2, NB, C], F32R)
        nat_lo = sb("nat_lo", [P, 2, NB, C], F32R)
        hT = sb("hT", [P, 2, N])
        hT_hi = sb("hT_hi", [P, 2, N], F32R)
        hT_lo = sb("hT_lo", [P, 2, N], F32R)
        S_hi = sb("S_hi", [P, 2, H], F32R)
        S_lo = sb("S_lo", [P, 2, H], F32R)
        work = sb("work", [P, 4, 2, H])
        r_sb, z_sb, t_sb, n_sb = (work[:, i] for i in range(4))
        wx_hi = sb("wx_hi", [P, L, G * C], F32R)
        wx_lo = sb("wx_lo", [P, L, G * C], F32R)
        wh_hi = sb("wh_hi", [P, L, G * C], F32R)
        wh_lo = sb("wh_lo", [P, L, G * C], F32R)
        ident = sb("ident", [P, P])
        ones = sb("ones", [P, P])
        rows = sb("rows", [P, 2, P])
        bias = sb("bias", [P, 2, L * G])
        bsum = sb("bsum", [P, L * G])
        mask = sb("mask", [P, B * NB])
        low = sb("low", [P, N], I32)
        lowf = sb("lowf", [P, 1])
        flag = sb("flag", [P, 1], I32)
        stats = sb("stats", [P, NB, 6])
        mv = sb("mv", [P, 2, NB, 2])
        vare = sb("vare", [P, 2, NB])
        mhalf = sb("mhalf", [P, NB])
        rstd = sb("rstd", [P, 2, NB])

        p_S = [ctx.enter_context(nc.psum_tensor(f"p_S{h}", [P, H], F32)) for h in range(2)]
        p_r = ctx.enter_context(nc.psum_tensor("p_r", [P, H], F32))
        p_z = ctx.enter_context(nc.psum_tensor("p_z", [P, H], F32))
        p_hn = ctx.enter_context(nc.psum_tensor("p_hn", [P, H], F32))
        p_xn = ctx.enter_context(nc.psum_tensor("p_xn", [P, H], F32))
        p_tr = [ctx.enter_context(nc.psum_tensor(f"p_tr{h}", [P, HB, P], F32)) for h in range(2)]
        p_start = [[p_S[0], p_S[1], p_r, p_z], [p_hn, p_xn, p_tr[0], p_tr[1]]]

        def flat(t):
            return t[:, :] if len(t.shape) == 2 else t[:, :, :].rearrange("p a b -> p (a b)")

        w_nat = work[:, 0].rearrange("p a b -> p (a b)")[:, 0:L * C].rearrange("p (l d) -> p l d", l=L)
        wih_nat = work[:, 1:3].rearrange("p a b c -> p (a b c)")[:, 0:L * G * C].rearrange("p (q d) -> p q d", q=L * G)
        whh_nat = hT[:, :, :].rearrange("p a b -> p (a b)")[:, 0:L * G * C].rearrange("p (q d) -> p q d", q=L * G)
        wT = y[:, 0].rearrange("p a b -> p (a b)")[:, 0:L * C]
        wihT = y[:, 1].rearrange("p a b -> p (a b)")[:, 0:2 * G * C]

        ident_zero = sem("ident_zero")
        ident_made = sem("ident_made")
        rows_in = sem("rows_in")
        w_in = sem("w_in")
        start_tr = sem("start_tr")
        start_copied = sem("start_copied")
        start_joined = sem("start_joined")
        start_hi = sem("start_hi")
        start_lo = sem("start_lo")
        rows_tr = sem("rows_tr")
        rows_out = sem("rows_out")
        adj_loaded = [sem(f"adj_loaded{j}") for j in range(NB)]
        adj_ready = sem("adj_ready")
        adj_checked = sem("adj_checked")
        low_zero = sem("low_zero")
        x_loaded = [sem(f"x_loaded{s}") for s in range(2)]
        y_loaded = [sem(f"y_loaded{s}") for s in range(2)]
        out_stored = [sem(f"out_stored{s}") for s in range(2)]
        xnat_hi = sem("xnat_hi")
        xnat_lo = sem("xnat_lo")
        x_tr = sem("x_tr")
        xT_hi = sem("xT_hi")
        xT_done = sem("xT_done")
        s_done = sem("s_done")
        s_hi_made = sem("s_hi_made")
        s_split = sem("s_split")
        hn_done = sem("hn_done")
        r_done = sem("r_done")
        xn_done = sem("xn_done")
        z_done = sem("z_done")
        r_act = sem("r_act")
        z_act = sem("z_act")
        t_mul = sem("t_mul")
        t_add = sem("t_add")
        n_act = sem("n_act")
        d_sub = sem("d_sub")
        d_mul = sem("d_mul")
        h_new = sem("h_new")
        h_hi_made = sem("h_hi_made")
        h_split = sem("h_split")
        h_tr = sem("h_tr")
        nat_hi_made = sem("nat_hi_made")
        nat_split = sem("nat_split")
        y_added = sem("y_added")
        y_stats = sem("y_stats")
        y_aggr = sem("y_aggr")
        var_eps = sem("var_eps")
        rstd_made = sem("rstd_made")
        y_normed = sem("y_normed")
        low_masked = sem("low_masked")
        low_red = sem("low_red")
        low_sum = sem("low_sum")
        flag_made = sem("flag_made")

        g_loaded = sem("g_loaded")
        g_xtr = sem("g_xtr")
        g_xT = sem("g_xT")
        g_s = sem("g_s")
        g_s_out = sem("g_s_out")
        g_gates = sem("g_gates")
        g_rz = sem("g_rz")
        g_n = sem("g_n")
        g_dve = sem("g_dve")
        g_tr = sem("g_tr")
        g_nat = sem("g_nat")
        g_added = sem("g_added")
        g_stats = sem("g_stats")
        g_aggr = sem("g_aggr")
        g_var = sem("g_var")
        g_rstd = sem("g_rstd")
        g_normed = sem("g_normed")
        CHAIN = 5
        g_S = x_in[:, 1].rearrange("p a b -> p (a b)")

        adj_v = adj.rearrange("b (j p) n -> b j p n", p=P)
        x_v = x.rearrange("b (j p) c -> b p j c", p=P)
        out_v = out.rearrange("b (j p) c -> b p j c", p=P)

        def pairs(eng, body):
            body(0, True, False)
            with eng.Fori(1, PAIRS - 1) as p:
                body(p, False, False)
            body(PAIRS - 1, False, True)

        def general(eng, body, stores=False):
            eng.wait_ge(flag_made, 1)
            with eng.If(eng.value_load(flag[0:1, 0:1], min_val=0, max_val=1) != 0):
                with eng.Fori(0, B) as b:
                    body(b)
                if stores:
                    eng.wait_ge(out_stored[1], 16 * (PAIRS + B))

        def half(h):
            return slice(h * H, (h + 1) * H)

        block = ctx.enter_context(nc.Block())

        @block.sync
        def _(sp):
            sp.dma_start(w_nat, weight.rearrange("l p d -> p l d")).then_inc(w_in, 16)
            sp.dma_start(wih_nat, w_ih.rearrange("l (q p) d -> p (l q) d", p=P)).then_inc(w_in, 16)
            sp.dma_start(whh_nat, w_hh.rearrange("l (q p) d -> p (l q) d", p=P)).then_inc(w_in, 16)
            sp.dma_start(rows[0:L * G, 0, :], b_ih.rearrange("l (q p) -> (l q) p", p=P)).then_inc(rows_in, 16)
            sp.dma_start(rows[L * G:2 * L * G, 0, :], b_hh.rearrange("l (q p) -> (l q) p", p=P)).then_inc(rows_in, 16)
            sp.dma_start(rows[0:B * NB, 1, :], nodemask.rearrange("b (j p) -> (b j) p", p=P)).then_inc(rows_in, 16)
            sp.dma_start(x_in[:, 0], x_v[0]).then_inc(x_loaded[0], 16)
            for j in range(NB):
                sp.dma_start(adj_in[:, j], adj_v[0, j]).then_inc(adj_loaded[j], 16)
            sp.dma_start(x_in[:, 1], x_v[1]).then_inc(x_loaded[1], 16)
            for j in range(NB):
                sp.wait_ge(adj_ready, j + 1)
                sp.wait_ge(adj_checked, j + 1)
                sp.dma_start(adj_in[:, j], adj_v[1, j]).then_inc(adj_loaded[j], 16)

            def next_adj(p, s):
                for j in range(NB):
                    sp.wait_ge(adj_checked, NB * (2 * p + 1 + s) + j + 1)
                    sp.wait_ge(adj_ready, NB * (2 * p + 1 + s) + j + 1)
                    sp.dma_start(adj_in[:, j], adj_v[2 * p + 2 + s, j]).then_inc(adj_loaded[j], 16)

            def store(p, s):
                sp.wait_ge(y_normed, 2 * p + s + 1)
                sp.dma_start(out_v[2 * p + s], y[:, s]).then_inc(out_stored[s], 16)

            def body(p, first, last):
                if first:
                    sp.wait_ge(start_joined, L)
                else:
                    store(p - 1, 1)
                for s in range(2):
                    if not first:
                        sp.wait_ge(out_stored[s], 16 * p)
                    sp.dma_start(y[:, s], x_v[2 * p + s]).then_inc(y_loaded[s], 16)
                if not last:
                    next_adj(p, 0)
                    for s in range(2):
                        sp.wait_ge(x_tr, 4 * p + 2 * s + 2)
                        sp.wait_ge(xnat_lo, 2 * p + s + 1)
                        sp.dma_start(x_in[:, s], x_v[2 * p + 2 + s]).then_inc(x_loaded[s], 16)
                    next_adj(p, 1)
                store(p, 0)

            pairs(sp, body)
            store(PAIRS - 1, 1)
            for s in range(2):
                sp.wait_ge(out_stored[s], 16 * PAIRS)

            def graph(b):
                sp.dma_start(adj_in[:, :, :], adj_v[b].rearrange("j p n -> p j n")).then_inc(g_loaded, 16)
                sp.dma_start(x_in[:, 0], x_v[b]).then_inc(g_loaded, 16)
                sp.wait_ge(out_stored[1], 16 * PAIRS + 16 * b)
                sp.dma_start(y[:, 0], x_v[b]).then_inc(g_loaded, 16)
                sp.wait_ge(g_normed, b + 1)
                sp.dma_start(out_v[b], y[:, 0]).then_inc(out_stored[1], 16)

            general(sp, graph, stores=True)

        @block.tensor
        def _(pe):
            pe.wait_ge(ident_made, 1)
            pe.wait_ge(w_in, 48)
            for l in range(L):
                pw, pi, ph, pj = p_start[l % 2]
                if l >= 2:
                    pe.wait_ge(start_lo, l - 1)
                nc.tensor.transpose(flat(pw)[:, 0:C], w_nat[:, l], ident[:, :])
                for q in range(G):
                    nc.tensor.transpose(flat(pi)[:, q * C:(q + 1) * C], wih_nat[:, G * l + q], ident[:, :])
                for q in range(G):
                    last = nc.tensor.transpose(flat(ph)[:, q * C:(q + 1) * C], whh_nat[:, G * l + q], ident[:, :])
                last.then_inc(start_tr, 1)
                pe.wait_ge(start_copied, l + 1)
                nc.tensor.matmul(flat(pj)[:, 0:G * C], wT[:, l * C:(l + 1) * C],
                                 wihT[:, (l % 2) * G * C:(l % 2 + 1) * G * C],
                                 start=True, stop=True).then_inc(start_joined, 1)
            pe.wait_ge(start_lo, L)
            pe.wait_ge(rows_in, 48)
            nc.tensor.transpose(p_r[:, 0:2 * L * G], rows[0:2 * L * G, 0, :], ident[0:2 * L * G, 0:2 * L * G])
            nc.tensor.transpose(p_z[:, 0:B * NB], rows[0:B * NB, 1, :], ident[0:B * NB, 0:B * NB]).then_inc(rows_tr, 1)
            pe.wait_ge(rows_out, 2)

            def transpose_x(p, s, first):
                pe.wait_ge(x_loaded[s], 16 * (p + 1))
                for h in range(2):
                    if not first:
                        pe.wait_ge(y_added, 4 * (p - 1) + 2 * s + h + 1)
                    elif s == 1:
                        pe.wait_ge(xT_done, h + 1)
                    for i in range(HB):
                        last = nc.tensor.transpose(p_tr[h][:, i, :], x_in[:, s, h * HB + i], ident[:, :])
                    last.then_inc(x_tr, 1)

            def transpose_h(p, g, h):
                pe.wait_ge(h_new, HS * p + 2 * g + h + 1)
                if g == STEPS - 1:
                    pass
                for i in range(HB):
                    n0 = h * H + i * P
                    last = nc.tensor.transpose(p_tr[h][:, i, :], hT[:, g % 2, n0:n0 + P], ident[:, :])
                last.then_inc(h_tr, 1)

            def aggregate(p, g):
                l, s = divmod(g, 2)
                if l == 0:
                    pe.wait_ge(xnat_lo, 2 * p + s + 1)
                else:
                    pe.wait_ge(nat_split, HS_IN * p + 2 * (g - 2) + 2)
                for h in range(2):
                    for j in range(NB):
                        if l == 0 and h == 0:
                            pe.wait_ge(adj_ready, NB * (2 * p + s) + j + 1)
                        for part in (nat_hi, nat_lo):
                            last = nc.tensor.matmul(p_S[h][:, :], part[:, s, j], adj_hi[:, s, j, half(h)],
                                                    start=(j == 0 and part is nat_hi),
                                                    stop=(j == NB - 1 and part is nat_lo))
                    last.then_inc(s_done, 1)

            def product(bank, w, l, q, v, start, stop):
                w_h, w_l = w
                v_h, v_l = v
                cols = slice(q * C, (q + 1) * C)
                nc.tensor.matmul(bank[:, :], w_h[:, l, cols], v_h, start=start, stop=False)
                nc.tensor.matmul(bank[:, :], w_h[:, l, cols], v_l, start=False, stop=False)
                return nc.tensor.matmul(bank[:, :], w_l[:, l, cols], v_h, start=False, stop=stop)

            def gates(p, g, h, first):
                l, s = divmod(g, 2)
                k = 2 * g + h
                if l == 0:
                    pe.wait_ge(xT_done, 4 * p + k + 1)
                else:
                    pe.wait_ge(h_split, HS_IN * p + k - 4 + 1)
                state = (hT_hi[:, s, half(h)], hT_lo[:, s, half(h)])
                fed = (S_hi[:, h], S_lo[:, h])
                prior = not (first and k == 0)
                if prior:
                    pe.wait_ge(r_act, HS * p + k)
                product(p_r, (wh_hi, wh_lo), l, 0, state, True, False)
                if prior:
                    pe.wait_ge(z_act, HS * p + k)
                product(p_z, (wh_hi, wh_lo), l, 1, state, True, False)
                if prior:
                    pe.wait_ge(t_mul, HS * p + k)
                product(p_hn, (wh_hi, wh_lo), l, 2, state, True, True).then_inc(hn_done, 1)
                pe.wait_ge(s_split, HS * p + k + 1)
                product(p_r, (wx_hi, wx_lo), l, 0, fed, False, True).then_inc(r_done, 1)
                if prior:
                    pe.wait_ge(t_add, HS * p + k)
                product(p_xn, (wx_hi, wx_lo), l, 2, fed, True, True).then_inc(xn_done, 1)
                product(p_z, (wx_hi, wx_lo), l, 1, fed, False, True).then_inc(z_done, 1)

            def transpose_former(p, g, h, first):
                if g == 0:
                    if not first:
                        pe.wait_ge(xT_done, 4 * p + h + 1)
                        transpose_h(p - 1, STEPS - 1, h)
                else:
                    if g == 1:
                        pe.wait_ge(xT_done, 4 * p + 2 + h + 1)
                    else:
                        pe.wait_ge(nat_split, HS_IN * p + 2 * (g - 2) + h + 1)
                    transpose_h(p, g - 1, h)

            def body(p, first, last):
                for g in range(STEPS):
                    if g < 2:
                        transpose_x(p, g, first)
                    aggregate(p, g)
                    for h in range(2):
                        transpose_former(p, g, h, first)
                        gates(p, g, h, first)

            pairs(pe, body)
            for h in range(2):
                pe.wait_ge(y_added, 4 * (PAIRS - 1) + h + 1)
                transpose_h(PAIRS - 1, STEPS - 1, h)
            pe.wait_ge(low_red, 1)
            nc.tensor.matmul(p_r[:, 0:1], ones[:, :], lowf[:, 0:1], start=True, stop=True).then_inc(low_sum, 1)

            def graph(b):
                pe.wait_ge(g_loaded, 48 * b + 48)
                for h in range(2):
                    for i in range(HB):
                        last = nc.tensor.transpose(p_tr[h][:, i, :], x_in[:, 0, h * HB + i], ident[:, :])
                    last.then_inc(g_xtr, 1)
                for l in range(L):
                    if l:
                        pe.wait_ge(g_nat, (L - 1) * b + l)
                    for h in range(2):
                        for j in range(NB):
                            last = nc.tensor.matmul(p_S[h][:, :], x_in[:, 0, j], adj_in[:, j, half(h)],
                                                    start=(j == 0), stop=(j == NB - 1))
                        last.then_inc(g_s, 1)
                    for h in range(2):
                        m = 2 * L * b + 2 * l + h
                        if l == 0:
                            pe.wait_ge(g_xT, 2 * b + h + 1)
                        if l or h:
                            pe.wait_ge(g_dve, CHAIN * m)
                        pe.wait_ge(g_s_out, m + 1)
                        for bank, q, fed, state in ((p_r, 0, True, True), (p_z, 1, True, True),
                                                    (p_hn, 2, False, True), (p_xn, 2, True, False)):
                            terms = []
                            if fed:
                                terms += [(w, g_S[:, half(h)]) for w in (wx_hi, wx_lo)]
                            if state:
                                terms += [(w, hT[:, 0, half(h)]) for w in (wh_hi, wh_lo)]
                            for n, (w, v) in enumerate(terms):
                                last = nc.tensor.matmul(bank[:, :], w[:, l, q * C:(q + 1) * C].bitcast(F32), v,
                                                        start=(n == 0), stop=(n == len(terms) - 1))
                        last.then_inc(g_gates, 1)
                    pe.wait_ge(g_dve, CHAIN * (2 * L * b + 2 * l + 2))
                    for j in range(NB):
                        last = nc.tensor.transpose(p_tr[j // HB][:, j % HB, :], hT[:, 0, j * P:(j + 1) * P], ident[:, :])
                    last.then_inc(g_tr, 1)

            general(pe, graph)

        @block.scalar
        def _(act):
            def copy(dst, src):
                return nc.scalar.activation(dst, src, ACT.Copy)

            for l in range(L):
                pw, pi, ph, pj = p_start[l % 2]
                act.wait_ge(start_tr, l + 1)
                copy(wh_hi[:, l], flat(ph)[:, 0:G * C])
                act.wait_ge(start_joined, l + 1)
                copy(wx_hi[:, l], flat(pj)[:, 0:G * C]).then_inc(start_hi, 1)

            def take_adj(p, s, j):
                act.wait_ge(adj_loaded[j], 16 * (2 * p + s + 1))
                copy(adj_hi[:, s, j], adj_in[:, j]).then_inc(adj_ready, 1)

            def split_x(p, s, first):
                act.wait_ge(x_loaded[s], 16 * (p + 1))
                if not first:
                    act.wait_ge(s_done, HS * (p - 1) + 2 * (STEPS - 2 + s) + 2)
                copy(nat_hi[:, s], x_in[:, s]).then_inc(xnat_hi, 1)

            def take_xT(p, s):
                for h in range(2):
                    act.wait_ge(x_tr, 4 * p + 2 * s + h + 1)
                    copy(hT[:, s, half(h)], flat(p_tr[h]))
                    copy(hT_hi[:, s, half(h)], flat(p_tr[h])).then_inc(xT_hi, 1)

            def take_former(p, g, h):
                act.wait_ge(h_tr, HS * p + 2 * g + h + 1)
                copy(nat_hi[:, g % 2, h * HB:(h + 1) * HB], p_tr[h][:, :, :]).then_inc(nat_hi_made, 1)

            def gate(dst, bank, done, made, func, b, p, k):
                act.wait_ge(done, HS * p + k + 1)
                nc.scalar.activation(dst, bank, func, bias=b).then_inc(made, 1)

            def s_high(p, g, h):
                act.wait_ge(s_done, HS * p + 2 * g + h + 1)
                copy(S_hi[:, h], p_S[h][:, :]).then_inc(s_hi_made, 1)

            def h_high(p, g, h):
                act.wait_ge(h_new, HS * p + 2 * g + h + 1)
                copy(hT_hi[:, g % 2, half(h)], hT[:, g % 2, half(h)]).then_inc(h_hi_made, 1)

            def body(p, first, last):
                for g in range(STEPS):
                    l, s = divmod(g, 2)
                    blocks = {0: ((p, 1), ((), (3, 4), (5, 6), (7,))),
                              STEPS - 2: ((p + 1, 0), ((), (0,), (1,), (2, 3, 4))),
                              STEPS - 1: ((p + 1, 0), ((5,), (6,), (7,), ()))}
                    graph_of, places = blocks.get(g, (None, ((),) * 4))
                    if last and g:
                        places = ((),) * 4

                    def fill(n):
                        for j in places[n]:
                            take_adj(*graph_of, j)

                    if l == 0:
                        take_xT(p, s)
                    s_high(p, g, 0)
                    if 1 <= g <= STEPS - 2:
                        h_high(p, g - 1, 1)
                    if g == 0:
                        split_x(p, 1, first)
                    elif g == STEPS - 1 and not last:
                        split_x(p + 1, 0, False)
                    fill(0)
                    s_high(p, g, 1)
                    if 1 <= g <= STEPS - 2:
                        take_former(p, g - 1, 0)
                    fill(1)
                    for h in range(2):
                        k = 2 * g + h
                        gate(r_sb[:, h], p_r[:, :], r_done, r_act, ACT.Sigmoid, bsum[:, G * l:G * l + 1], p, k)
                        gate(z_sb[:, h], p_z[:, :], z_done, z_act, ACT.Sigmoid, bsum[:, G * l + 1:G * l + 2], p, k)
                        if h == 0 and 1 <= g <= STEPS - 2:
                            take_former(p, g - 1, 1)
                        gate(n_sb[:, h], t_sb[:, h], t_add, n_act, ACT.Tanh, bias[:, 0, G * l + 2:G * l + 3], p, k)
                        if h == 0:
                            fill(2)
                    if l < L - 1:
                        h_high(p, g, 0)
                    fill(3)
                    if g == STEPS - 1 and not last:
                        for j in range(3):
                            take_adj(p + 1, 1, j)

            split_x(0, 0, True)
            for j in range(NB):
                take_adj(0, 0, j)
            for j in range(3):
                take_adj(0, 1, j)
            act.wait_ge(rows_out, 2)
            pairs(act, body)

            def graph(b):
                for h in range(2):
                    act.wait_ge(g_xtr, 2 * b + h + 1)
                    copy(hT[:, 0, half(h)], flat(p_tr[h])).then_inc(g_xT, 1)
                for l in range(L):
                    for h in range(2):
                        act.wait_ge(g_s, 2 * L * b + 2 * l + h + 1)
                        copy(g_S[:, half(h)], p_S[h][:, :]).then_inc(g_s_out, 1)
                    for h in range(2):
                        m = 2 * L * b + 2 * l + h
                        act.wait_ge(g_gates, m + 1)
                        nc.scalar.activation(r_sb[:, 0], p_r[:, :], ACT.Sigmoid, bias=bsum[:, G * l:G * l + 1])
                        nc.scalar.activation(z_sb[:, 0], p_z[:, :], ACT.Sigmoid,
                                             bias=bsum[:, G * l + 1:G * l + 2]).then_inc(g_rz, 1)
                        act.wait_ge(g_dve, CHAIN * m + 2)
                        nc.scalar.activation(n_sb[:, 0], t_sb[:, 0], ACT.Tanh,
                                             bias=bias[:, 0, G * l + 2:G * l + 3]).then_inc(g_n, 1)

            general(act, graph)

        @block.vector
        def _(dve):
            def lo(dst, src, hi):
                return nc.vector.tensor_tensor(dst, src, hi.bitcast(F32), ALU.subtract)

            nc.vector.memset(ones[:, :], 1.0)
            nc.vector.memset(low[:, :], 0).then_inc(low_zero, 1)
            dve.wait_ge(low_zero, 1)
            for l in range(L):
                pw, pi, ph, pj = p_start[l % 2]
                dve.wait_ge(start_tr, l + 1)
                if l >= 2:
                    dve.wait_ge(start_joined, l - 1)
                nc.vector.tensor_copy(wT[:, l * C:(l + 1) * C], flat(pw)[:, 0:C])
                nc.vector.tensor_copy(wihT[:, (l % 2) * G * C:(l % 2 + 1) * G * C],
                                      flat(pi)[:, 0:G * C]).then_inc(start_copied, 1)
                dve.wait_ge(start_hi, l + 1)
                lo(wh_lo[:, l], flat(ph)[:, 0:G * C], wh_hi[:, l])
                lo(wx_lo[:, l], flat(pj)[:, 0:G * C], wx_hi[:, l]).then_inc(start_lo, 1)
            dve.wait_ge(rows_tr, 1)
            nc.vector.tensor_copy(bias[:, :, :].rearrange("p a b -> p (a b)"), p_r[:, 0:2 * L * G]).then_inc(rows_out, 1)
            nc.vector.tensor_copy(mask[:, :], p_z[:, 0:B * NB])
            dve.wait_ge(rows_out, 1)
            nc.vector.tensor_tensor(bsum[:, :], bias[:, 0], bias[:, 1], ALU.add).then_inc(rows_out, 1)

            def check_adj(p, s, j, first=False):
                dve.wait_ge(adj_loaded[j], 16 * (2 * p + s + 1))
                if not (first and s == 0 and j == 0):
                    dve.wait_ge(adj_checked, NB * (2 * p + s) + j)
                nc.vector.tensor_tensor(low[:, :], low[:, :], adj_in[:, j].bitcast(I32),
                                        ALU.bitwise_or).then_inc(adj_checked, 1)

            def split_x(p, s):
                dve.wait_ge(xnat_hi, 2 * p + s + 1)
                lo(nat_lo[:, s], x_in[:, s], nat_hi[:, s]).then_inc(xnat_lo, 1)

            def take_xT(p, s):
                for h in range(2):
                    dve.wait_ge(xT_hi, 4 * p + 2 * s + h + 1)
                    lo(hT_lo[:, s, half(h)], flat(p_tr[h]), hT_hi[:, s, half(h)]).then_inc(xT_done, 1)

            def take_former(p, g, h):
                dve.wait_ge(nat_hi_made, HS_IN * p + 2 * g + h + 1)
                lo(nat_lo[:, g % 2, h * HB:(h + 1) * HB], p_tr[h][:, :, :],
                   nat_hi[:, g % 2, h * HB:(h + 1) * HB]).then_inc(nat_split, 1)

            def residual(p, s, h):
                if h == 0:
                    dve.wait_ge(y_loaded[s], 16 * (p + 1))
                dve.wait_ge(h_tr, HS * p + 2 * (STEPS - 2 + s) + h + 1)
                for i in range(HB):
                    j = h * HB + i
                    col = NB * (2 * p + s) + j
                    last = nc.vector.scalar_tensor_tensor(y[:, s, j], p_tr[h][:, i, :], mask[:, bass.ds(col, 1)],
                                                          y[:, s, j], ALU.mult, ALU.add)
                last.then_inc(y_added, 1)
                dve.wait_ge(y_added, 4 * p + 2 * s + h + 1)
                for i in range(HB):
                    j = h * HB + i
                    last = nc.vector.bn_stats(stats[:, j], y[:, s, j])
                last.then_inc(y_stats, 1)

            def wait_stats(p, s, h):
                dve.wait_ge(y_stats, 4 * p + 2 * s + h + 1)

            def moments(s, h):
                for j in range(h * HB, (h + 1) * HB):
                    last = nc.vector.bn_aggr(mv[:, s, j], stats[:, j])
                if h == 1:
                    last.then_inc(y_aggr, 1)

            def variance_eps(p, s):
                dve.wait_ge(y_aggr, 2 * p + s + 1)
                nc.vector.tensor_scalar(vare[:, s], mv[:, s, :, 1], EPS, None, ALU.add).then_inc(var_eps, 1)

            def normalise(p, s):
                dve.wait_ge(rstd_made, 2 * p + s + 1)
                for j in range(NB):
                    last = nc.vector.tensor_scalar(y[:, s, j], y[:, s, j], mv[:, s, j, 0:1], rstd[:, s, j:j + 1],
                                                   ALU.subtract, ALU.mult)
                last.then_inc(y_normed, 1)

            def s_low(p, g, h):
                dve.wait_ge(s_hi_made, HS * p + 2 * g + h + 1)
                lo(S_lo[:, h], p_S[h][:, :], S_hi[:, h]).then_inc(s_split, 1)

            def new_state(p, g, h):
                dve.wait_ge(d_mul, HS * p + 2 * g + h + 1)
                nc.vector.tensor_tensor(hT[:, g % 2, half(h)], n_sb[:, h], t_sb[:, h], ALU.add).then_inc(h_new, 1)

            def h_low(p, g, h):
                dve.wait_ge(h_hi_made, HS_IN * p + 2 * g + h + 1)
                lo(hT_lo[:, g % 2, half(h)], hT[:, g % 2, half(h)], hT_hi[:, g % 2, half(h)]).then_inc(h_split, 1)

            def body(p, first, last):
                checks = [(p, 1, j) for j in range(NB)] + [(p + 1, 0, j) for j in range(NB) if not last]

                def fill(g):
                    if g and checks:
                        check_adj(*checks.pop(0))

                for g in range(STEPS):
                    l, s = divmod(g, 2)
                    ended = (p, 0) if g == STEPS - 1 else (p - 1, 1) if g == 0 and not first else None
                    if g:
                        new_state(p, g - 1, 1)
                    elif not first:
                        new_state(p - 1, STEPS - 1, 1)
                    if l == 0:
                        take_xT(p, s)
                    s_low(p, g, 0)
                    if 1 <= g <= STEPS - 2:
                        h_low(p, g - 1, 1)
                    if g == 0:
                        split_x(p, 1)
                    elif g == STEPS - 1 and not last:
                        split_x(p + 1, 0)
                    fill(g)
                    s_low(p, g, 1)
                    for h in range(2):
                        k = 2 * g + h
                        if h == 0:
                            if ended:
                                residual(*ended, 0)
                                wait_stats(*ended, 0)
                            elif g:
                                take_former(p, g - 1, 0)
                        dve.wait_ge(hn_done, HS * p + k + 1)
                        dve.wait_ge(r_act, HS * p + k + 1)
                        nc.vector.scalar_tensor_tensor(t_sb[:, h], p_hn[:, :], bias[:, 1, G * l + 2:G * l + 3],
                                                       r_sb[:, h], ALU.add, ALU.mult).then_inc(t_mul, 1)
                        if ended:
                            moments(ended[1], h)
                        dve.wait_ge(xn_done, HS * p + k + 1)
                        dve.wait_ge(t_mul, HS * p + k + 1)
                        nc.vector.tensor_tensor(t_sb[:, h], p_xn[:, :], t_sb[:, h], ALU.add).then_inc(t_add, 1)
                        if h == 0:
                            if ended:
                                residual(*ended, 1)
                                wait_stats(*ended, 1)
                            elif g:
                                take_former(p, g - 1, 1)
                            fill(g)
                    if ended:
                        variance_eps(*ended)
                    new_state(p, g, 0)
                    if l < L - 1:
                        h_low(p, g, 0)
                    fill(g)
                    if g == 0 and not first:
                        normalise(p - 1, 1)
                    elif g == STEPS - 1:
                        normalise(p, 0)

            split_x(0, 0)
            for j in range(NB):
                check_adj(0, 0, j, True)
            pairs(dve, body)
            new_state(PAIRS - 1, STEPS - 1, 1)
            for h in range(2):
                residual(PAIRS - 1, 1, h)
                wait_stats(PAIRS - 1, 1, h)
                moments(1, h)
            variance_eps(PAIRS - 1, 1)
            normalise(PAIRS - 1, 1)

            dve.wait_ge(adj_checked, B * NB)
            nc.vector.tensor_scalar(low[:, :], low[:, :], LOWBITS, None, ALU.bitwise_and).then_inc(low_masked, 1)
            dve.wait_ge(low_masked, 1)
            nc.vector.tensor_reduce(lowf[:, :], low[:, :], AX.X, ALU.max).then_inc(low_red, 1)
            dve.wait_ge(low_sum, 1)
            nc.vector.tensor_scalar(flag[:, :], p_r[:, 0:1], 0.0, None, ALU.is_gt).then_inc(flag_made, 1)

            def graph(b):
                for l in range(L):
                    for h in range(2):
                        m = 2 * L * b + 2 * l + h
                        n, t, z = n_sb[:, 0], t_sb[:, 0], z_sb[:, 0]
                        dve.wait_ge(g_rz, m + 1)
                        nc.vector.scalar_tensor_tensor(t, p_hn[:, :], bias[:, 1, G * l + 2:G * l + 3],
                                                       r_sb[:, 0], ALU.add, ALU.mult).then_inc(g_dve, 1)
                        dve.wait_ge(g_dve, CHAIN * m + 1)
                        nc.vector.tensor_tensor(t, p_xn[:, :], t, ALU.add).then_inc(g_dve, 1)
                        dve.wait_ge(g_n, m + 1)
                        nc.vector.tensor_tensor(t, hT[:, 0, half(h)], n, ALU.subtract).then_inc(g_dve, 1)
                        dve.wait_ge(g_dve, CHAIN * m + 3)
                        nc.vector.tensor_tensor(t, z, t, ALU.mult).then_inc(g_dve, 1)
                        dve.wait_ge(g_dve, CHAIN * m + 4)
                        nc.vector.tensor_tensor(hT[:, 0, half(h)], n, t, ALU.add).then_inc(g_dve, 1)
                    dve.wait_ge(g_tr, L * b + l + 1)
                    for h in range(2):
                        if l < L - 1:
                            last = nc.vector.tensor_copy(x_in[:, 0, h * HB:(h + 1) * HB], p_tr[h][:, :, :])
                        if l == L - 1:
                            for i in range(HB):
                                j = h * HB + i
                                last = nc.vector.scalar_tensor_tensor(
                                    y[:, 0, j], p_tr[h][:, i, :], mask[:, bass.ds(NB * b + j, 1)], y[:, 0, j],
                                    ALU.mult, ALU.add)
                    last.then_inc(g_nat if l < L - 1 else g_added, 1)
                dve.wait_ge(g_added, b + 1)
                for j in range(NB):
                    last = nc.vector.bn_stats(stats[:, j], y[:, 0, j])
                last.then_inc(g_stats, 1)
                dve.wait_ge(ident_made, 1)
                dve.wait_ge(g_stats, b + 1)
                for j in range(NB):
                    last = nc.vector.bn_aggr(mv[:, 0, j], stats[:, j])
                last.then_inc(g_aggr, 1)
                dve.wait_ge(g_aggr, b + 1)
                nc.vector.tensor_scalar(vare[:, 0], mv[:, 0, :, 1], EPS, None, ALU.add).then_inc(g_var, 1)
                dve.wait_ge(g_rstd, b + 1)
                for j in range(NB):
                    last = nc.vector.tensor_scalar(y[:, 0, j], y[:, 0, j], mv[:, 0, j, 0:1], rstd[:, 0, j:j + 1],
                                                   ALU.subtract, ALU.mult)
                last.then_inc(g_normed, 1)

            general(dve, graph)

        @block.gpsimd
        def _(pool):
            nc.gpsimd.memset(ident[:, :], 0.0).then_inc(ident_zero, 1)
            pool.wait_ge(ident_zero, 1)
            nc.gpsimd.affine_select(out=ident[:, :], in_=ident[:, :], compare_op=ALU.not_equal, fill=1.0,
                                    base=0, pattern=[[-1, P]], channel_multiplier=1).then_inc(ident_made, 1)
            nc.gpsimd.memset(mhalf[:, :], -0.5)

            def inverse_deviation(p, s):
                pool.wait_ge(var_eps, 2 * p + s + 1)
                nc.gpsimd.tensor_tensor(rstd[:, s], vare[:, s], mhalf[:, :], ALU.pow).then_inc(rstd_made, 1)

            def body(p, first, last):
                for g in range(STEPS):
                    l, s = divmod(g, 2)
                    for h in range(2):
                        k = 2 * g + h
                        if h == 1 and g == 0 and not first:
                            inverse_deviation(p - 1, 1)
                        if h == 1 and g == STEPS - 1:
                            inverse_deviation(p, 0)
                        pool.wait_ge(n_act, HS * p + k + 1)
                        nc.gpsimd.tensor_tensor(t_sb[:, h], hT[:, s, half(h)], n_sb[:, h],
                                                ALU.subtract).then_inc(d_sub, 1)
                        pool.wait_ge(d_sub, HS * p + k + 1)
                        nc.gpsimd.tensor_tensor(t_sb[:, h], z_sb[:, h], t_sb[:, h],
                                                ALU.mult).then_inc(d_mul, 1)

            pairs(pool, body)
            inverse_deviation(PAIRS - 1, 1)

            def graph(b):
                pool.wait_ge(g_var, b + 1)
                nc.gpsimd.tensor_tensor(rstd[:, 0], vare[:, 0], mhalf[:, :], ALU.pow).then_inc(g_rstd, 1)

            general(pool, graph)


_INS = ['x', 'adj', 'nodemask', 'L0_gnn_weight', 'L0_gnn_w_ih', 'L0_gnn_w_hh', 'L0_gnn_b_ih', 'L0_gnn_b_hh']


def kernel(**inputs):
    import numpy as _np
    import concourse.bacc as _bacc
    from concourse import mybir as _mybir
    from concourse.bass_utils import run_bass_kernel_spmd as _run

    nc = _bacc.Bacc("TRN2", target_bir_lowering=False, num_devices=1)
    arrays, args = {}, []
    for name in _INS:
        a = _np.ascontiguousarray(inputs[name])
        arrays[f"in_{name}_dram"] = a
        args.append(nc.dram_tensor(f"in_{name}_dram", a.shape, _mybir.dt.from_np(a.dtype), kind="ExternalInput").ap())
    out = nc.dram_tensor("out_0_dram", inputs["x"].shape, _mybir.dt.float32, kind="ExternalOutput").ap()
    gnn_kernel(nc, *args, out)
    r = _run(nc, [arrays], core_ids=[0])
    return r.results[0]["out_0_dram"]
```

```python
from contextlib import ExitStack

import concourse.bass as bass
from concourse import mybir

F32 = mybir.dt.float32
F32R = mybir.dt.float32r
I32 = mybir.dt.int32
ALU = mybir.AluOpType
ACT = mybir.ActivationFunctionType
AX = mybir.AxisListType

P = 128
EPS = 1e-5


def gnn_kernel(nc, x, adj, nodemask, weight, w_ih, w_hh, b_ih, b_hh, out):
    B, N, C = x.shape
    L = weight.shape[0]
    NB = N // P
    H = N // 2
    HB = NB // 2
    G = 3
    PAIRS = B // 2
    STEPS = 2 * L
    HS = 2 * STEPS
    HS_IN = HS - 4
    LOWBITS = 0xFFF

    ctx = ExitStack()
    with ctx:
        def sb(name, shape, dt=F32):
            return ctx.enter_context(nc.sbuf_tensor(name, shape, dt))

        def sem(name):
            return ctx.enter_context(nc.semaphore(name))

        adj_hi = sb("adj_hi", [P, 2, NB, N], F32R)
        adj_in = sb("adj_in", [P, NB, N])
        x_in = sb("x_in", [P, 2, NB, C])
        y = sb("y", [P, 2, NB, C])
        nat_hi = sb("nat_hi", [P, 2, NB, C], F32R)
        nat_lo = sb("nat_lo", [P, 2, NB, C], F32R)
        hT = sb("hT", [P, 2, N])
        hT_hi = sb("hT_hi", [P, 2, N], F32R)
        hT_lo = sb("hT_lo", [P, 2, N], F32R)
        S_hi = sb("S_hi", [P, 2, H], F32R)
        S_lo = sb("S_lo", [P, 2, H], F32R)
        work = sb("work", [P, 4, 2, H])
        r_sb, z_sb, t_sb, n_sb = (work[:, i] for i in range(4))
        wx_hi = sb("wx_hi", [P, L, G * C], F32R)
        wx_lo = sb("wx_lo", [P, L, G * C], F32R)
        wh_hi = sb("wh_hi", [P, L, G * C], F32R)
        wh_lo = sb("wh_lo", [P, L, G * C], F32R)
        ident = sb("ident", [P, P])
        ones = sb("ones", [P, 1])
        act_scratch = sb("act_scratch", [P, 1])
        bias = sb("bias", [P, 2, L * G])
        bsum = sb("bsum", [P, L * G])
        mask = sb("mask", [P, B * NB])
        low = sb("low", [P, N], I32)
        lowf = sb("lowf", [P, 1])
        flag = sb("flag", [P, 1], I32)
        stats = sb("stats", [P, NB, 6])
        mv = sb("mv", [P, 2, NB, 2])
        vare = sb("vare", [P, 2, NB])
        mhalf = sb("mhalf", [P, NB])
        rstd = sb("rstd", [P, 2, NB])
        shift = sb("shift", [P, NB])

        p_S = [ctx.enter_context(nc.psum_tensor(f"p_S{h}", [P, H], F32)) for h in range(2)]
        p_r = ctx.enter_context(nc.psum_tensor("p_r", [P, H], F32))
        p_z = ctx.enter_context(nc.psum_tensor("p_z", [P, H], F32))
        p_hn = ctx.enter_context(nc.psum_tensor("p_hn", [P, H], F32))
        p_xn = ctx.enter_context(nc.psum_tensor("p_xn", [P, H], F32))
        p_tr = [ctx.enter_context(nc.psum_tensor(f"p_tr{h}", [P, HB, P], F32)) for h in range(2)]
        p_start = [(p_r, p_z), (p_S[0], p_S[1]), (p_hn, p_xn), (p_r, p_z)]
        p_rows = p_start[L - 1][1][:, G * C:]

        def flat(t):
            return t[:, :, :].rearrange("p a b -> p (a b)")

        places_start = [work[:, 0:2].rearrange("p a b c -> p (a b c)")[:, 0:N], hT[:, 1],
                        y[:, 0].rearrange("p a b -> p (a b)"), y[:, 1].rearrange("p a b -> p (a b)")]
        w_nat = [t[:, 0:(1 + 2 * G) * C].rearrange("p (q d) -> p q d", d=C) for t in places_start]
        w_tr = work[:, 2:4].rearrange("p a b c -> p (a b c)")[:, 0:L * (1 + G) * C].rearrange("p (l d) -> p l d", l=L)
        bias_rows, mask_rows = (t[:, N - P:N] for t in places_start[0:2])

        ident_zero = sem("ident_zero")
        ident_made = sem("ident_made")
        rows_in = sem("rows_in")
        w_in = [sem(f"w_in{l}") for l in range(L)]
        start_tr = sem("start_tr")
        start_copied = sem("start_copied")
        start_joined = sem("start_joined")
        start_hi = sem("start_hi")
        start_lo = sem("start_lo")
        rows_out = sem("rows_out")
        adj_loaded = [sem(f"adj_loaded{j}") for j in range(NB)]
        adj_ready = sem("adj_ready")
        adj_checked = sem("adj_checked")
        adj1_ready = sem("adj1_ready")
        low_zero = sem("low_zero")
        ones_made = sem("ones_made")
        x_loaded = [sem(f"x_loaded{s}") for s in range(2)]
        y_loaded = [sem(f"y_loaded{s}") for s in range(2)]
        out_stored = [sem(f"out_stored{s}") for s in range(2)]
        xnat_hi = sem("xnat_hi")
        xnat_lo = sem("xnat_lo")
        x_tr = sem("x_tr")
        xT_hi = sem("xT_hi")
        xT_done = sem("xT_done")
        xT_whole = sem("xT_whole")
        s_done = sem("s_done")
        s_hi_made = sem("s_hi_made")
        s_split = sem("s_split")
        hn_done = sem("hn_done")
        r_done = sem("r_done")
        xn_done = sem("xn_done")
        z_done = sem("z_done")
        r_act = sem("r_act")
        z_act = sem("z_act")
        t_mul = sem("t_mul")
        t_add = sem("t_add")
        n_act = sem("n_act")
        d_sub = sem("d_sub")
        d_mul = sem("d_mul")
        h_new = sem("h_new")
        h_hi_made = sem("h_hi_made")
        h_split = sem("h_split")
        h_tr = sem("h_tr")
        nat_hi_made = sem("nat_hi_made")
        nat_split = sem("nat_split")
        y_added = sem("y_added")
        y_stats = sem("y_stats")
        y_aggr = sem("y_aggr")
        var_eps = sem("var_eps")
        rstd_made = sem("rstd_made")
        y_normed = sem("y_normed")
        shift_made = sem("shift_made")
        y0_normed = sem("y0_normed")
        low_masked = sem("low_masked")
        low_red = sem("low_red")
        low_sum = sem("low_sum")
        flag_made = sem("flag_made")

        g_loaded = sem("g_loaded")
        g_xtr = sem("g_xtr")
        g_xT = sem("g_xT")
        g_s = sem("g_s")
        g_s_out = sem("g_s_out")
        g_gates = sem("g_gates")
        g_rz = sem("g_rz")
        g_n = sem("g_n")
        g_dve = sem("g_dve")
        g_tr = sem("g_tr")
        g_nat = sem("g_nat")
        g_added = sem("g_added")
        g_stats = sem("g_stats")
        g_aggr = sem("g_aggr")
        g_var = sem("g_var")
        g_rstd = sem("g_rstd")
        g_normed = sem("g_normed")
        CHAIN = 5
        g_S = x_in[:, 1].rearrange("p a b -> p (a b)")

        adj_v = adj.rearrange("b (j p) n -> b j p n", p=P)
        x_v = x.rearrange("b (j p) c -> b p j c", p=P)
        out_v = out.rearrange("b (j p) c -> b p j c", p=P)

        def pairs(eng, body):
            body(0, True, False)
            with eng.Fori(1, PAIRS - 1) as p:
                body(p, False, False)
            body(PAIRS - 1, False, True)

        def general(eng, body, stores=False):
            eng.wait_ge(y_normed, B)
            eng.wait_ge(y0_normed, 1)
            eng.wait_ge(flag_made, 1)
            with eng.If(eng.value_load(flag[0:1, 0:1], min_val=0, max_val=1) != 0):
                with eng.Fori(0, B) as b:
                    body(b)
                if stores:
                    eng.wait_ge(out_stored[1], 16 * (PAIRS + 1 + B))

        def half(h):
            return slice(h * H, (h + 1) * H)

        def wait_adj(eng, graph, j, graph1=False):
            if graph1:
                if j % 2:
                    eng.wait_ge(adj1_ready, j // 2 + 1)
                else:
                    eng.wait_ge(adj_ready, NB + j + 2)
            else:
                eng.wait_ge(adj_ready, NB * graph + j + 1)

        block = ctx.enter_context(nc.Block())

        @block.sync
        def _(sp):
            def load_layer(l):
                sp.dma_start(w_nat[l][:, 0], weight[l]).then_inc(w_in[l], 16)
                sp.dma_start(w_nat[l][:, 1:1 + G], w_ih[l].rearrange("(q p) d -> p q d", p=P)).then_inc(w_in[l], 16)
                sp.dma_start(w_nat[l][:, 1 + G:], w_hh[l].rearrange("(q p) d -> p q d", p=P)).then_inc(w_in[l], 16)

            for l in range(L):
                load_layer(l)
            sp.dma_start(bias_rows[0:L * G], b_ih.rearrange("l (q p) -> (l q) p", p=P)).then_inc(rows_in, 16)
            sp.dma_start(bias_rows[L * G:2 * L * G], b_hh.rearrange("l (q p) -> (l q) p", p=P)).then_inc(rows_in, 16)
            sp.dma_start(mask_rows[0:B * NB], nodemask.rearrange("b (j p) -> (b j) p", p=P)).then_inc(rows_in, 16)
            sp.dma_start(x_in[:, 0], x_v[0]).then_inc(x_loaded[0], 16)
            for j in range(NB):
                sp.dma_start(adj_in[:, j], adj_v[0, j]).then_inc(adj_loaded[j], 16)
            sp.dma_start(x_in[:, 1], x_v[1]).then_inc(x_loaded[1], 16)
            for j in range(NB):
                wait_adj(sp, 0, j)
                sp.wait_ge(adj_checked, j + 1)
                sp.dma_start(adj_in[:, j], adj_v[1, j]).then_inc(adj_loaded[j], 16)

            def next_adj(p, s, first):
                for j in range(NB):
                    sp.wait_ge(adj_checked, NB * (2 * p + 1 + s) + j + 1)
                    wait_adj(sp, 2 * p + 1 + s, j, first and s == 0)
                    sp.dma_start(adj_in[:, j], adj_v[2 * p + 2 + s, j]).then_inc(adj_loaded[j], 16)

            def store(p, s):
                sp.wait_ge(y_normed, 2 * p + s + 1)
                sp.dma_start(out_v[2 * p + s], y[:, s]).then_inc(out_stored[s], 16)

            def body(p, first, last):
                if first:
                    sp.wait_ge(start_tr, L)
                else:
                    store(p - 1, 1)
                for s in range(2):
                    if not first:
                        sp.wait_ge(out_stored[s], 16 * p)
                    sp.dma_start(y[:, s], x_v[2 * p + s]).then_inc(y_loaded[s], 16)
                if not last:
                    next_adj(p, 0, first)
                    for s in range(2):
                        sp.wait_ge(x_tr, 4 * p + 2 * s + 2)
                        sp.wait_ge(xnat_lo, 2 * p + s + 1)
                        sp.dma_start(x_in[:, s], x_v[2 * p + 2 + s]).then_inc(x_loaded[s], 16)
                    next_adj(p, 1, first)
                    store(p, 0)

            pairs(sp, body)
            sp.wait_ge(y0_normed, 1)
            sp.dma_start(out_v[B - 2], y[:, 0]).then_inc(out_stored[0], 16)
            for h in range(2):
                sp.wait_ge(y_normed, B - 1 + h)
                sp.dma_start(out_v[B - 1][:, h * HB:(h + 1) * HB],
                             y[:, 1, h * HB:(h + 1) * HB]).then_inc(out_stored[1], 16)
            sp.wait_ge(out_stored[0], 16 * PAIRS)
            sp.wait_ge(out_stored[1], 16 * (PAIRS + 1))

            def graph(b):
                sp.dma_start(adj_in[:, :, :], adj_v[b].rearrange("j p n -> p j n")).then_inc(g_loaded, 16)
                sp.dma_start(x_in[:, 0], x_v[b]).then_inc(g_loaded, 16)
                sp.wait_ge(out_stored[1], 16 * (PAIRS + 1) + 16 * b)
                sp.dma_start(y[:, 0], x_v[b]).then_inc(g_loaded, 16)
                sp.wait_ge(g_normed, b + 1)
                sp.dma_start(out_v[b], y[:, 0]).then_inc(out_stored[1], 16)

            general(sp, graph, stores=True)

        @block.tensor
        def _(pe):
            pe.wait_ge(ident_made, 1)

            def transpose_weights(l):
                px, ph = p_start[l]
                pe.wait_ge(w_in[l], 48)
                if l == L - 1:
                    pe.wait_ge(start_lo, 1)
                for q in range(G):
                    nc.tensor.transpose(px[:, q * C:(q + 1) * C], w_nat[l][:, 1 + q], ident[:, :])
                nc.tensor.transpose(px[:, G * C:(G + 1) * C], w_nat[l][:, 0], ident[:, :])
                if l == L - 1:
                    pe.wait_ge(rows_in, 48)
                    nc.tensor.transpose(p_rows[:, 0:2 * L * G], bias_rows[0:2 * L * G],
                                        ident[0:2 * L * G, 0:2 * L * G])
                    nc.tensor.transpose(p_rows[:, 2 * L * G:2 * L * G + B * NB], mask_rows[0:B * NB],
                                        ident[0:B * NB, 0:B * NB])
                for q in range(G):
                    last = nc.tensor.transpose(ph[:, q * C:(q + 1) * C], w_nat[l][:, 1 + G + q], ident[:, :])
                last.then_inc(start_tr, 1)

            def join_weights(l):
                pe.wait_ge(start_copied, l + 1)
                nc.tensor.matmul(p_start[l][0][:, 0:G * C], w_tr[:, l, G * C:], w_tr[:, l, 0:G * C],
                                 start=True, stop=True).then_inc(start_joined, 1)

            def transpose_x(p, s, first):
                pe.wait_ge(x_loaded[s], 16 * (p + 1))
                for h in range(2):
                    if not first:
                        pe.wait_ge(y_added, 4 * (p - 1) + 2 * s + h + 1)
                    elif s == 1:
                        pe.wait_ge(xT_done, h + 1)
                    for i in range(HB):
                        last = nc.tensor.transpose(p_tr[h][:, i, :], x_in[:, s, h * HB + i], ident[:, :])
                    last.then_inc(x_tr, 1)

            transpose_weights(0)
            transpose_weights(1)
            join_weights(0)
            transpose_weights(2)
            join_weights(1)
            transpose_weights(3)
            join_weights(2)
            transpose_x(0, 0, True)
            join_weights(3)
            pe.wait_ge(start_lo, 2)

            def transpose_h(p, g, h):
                pe.wait_ge(h_new, HS * p + 2 * g + h + 1)
                for i in range(HB):
                    n0 = h * H + i * P
                    last = nc.tensor.transpose(p_tr[h][:, i, :], hT[:, g % 2, n0:n0 + P], ident[:, :])
                last.then_inc(h_tr, 1)

            def aggregate(p, g, first):
                l, s = divmod(g, 2)
                if first and l == 0:
                    pe.wait_ge(xnat_lo, s + 1)
                    for j in range(NB):
                        wait_adj(pe, s, j, s == 1)
                        for h in range(2):
                            nc.tensor.matmul(p_S[h][:, :], nat_hi[:, s, j], adj_hi[:, s, j, half(h)],
                                             start=(j == 0), stop=False)
                            last = nc.tensor.matmul(p_S[h][:, :], nat_lo[:, s, j], adj_hi[:, s, j, half(h)],
                                                    start=False, stop=(j == NB - 1))
                            if j == NB - 1:
                                last.then_inc(s_done, 1)
                    return
                if l == 0:
                    pe.wait_ge(xnat_lo, 2 * p + s + 1)
                else:
                    pe.wait_ge(nat_split, HS_IN * p + 2 * (g - 2) + 2)
                for h in range(2):
                    for j in range(NB):
                        if l == 0 and h == 0:
                            wait_adj(pe, 2 * p + s, j)
                        for part in (nat_hi, nat_lo):
                            last = nc.tensor.matmul(p_S[h][:, :], part[:, s, j], adj_hi[:, s, j, half(h)],
                                                    start=(j == 0 and part is nat_hi),
                                                    stop=(j == NB - 1 and part is nat_lo))
                    last.then_inc(s_done, 1)

            def product(bank, w, l, q, v, start, stop):
                w_h, w_l = w
                v_h, v_l = v
                cols = slice(q * C, (q + 1) * C)
                nc.tensor.matmul(bank[:, :], w_h[:, l, cols], v_h, start=start, stop=False)
                nc.tensor.matmul(bank[:, :], w_h[:, l, cols], v_l, start=False, stop=False)
                return nc.tensor.matmul(bank[:, :], w_l[:, l, cols], v_h, start=False, stop=stop)

            def gates(p, g, h, first):
                l, s = divmod(g, 2)
                k = 2 * g + h
                if l == 0:
                    pe.wait_ge(xT_done, 4 * p + k + 1)
                else:
                    pe.wait_ge(h_split, HS_IN * p + k - 4 + 1)
                state = (hT_hi[:, s, half(h)], hT_lo[:, s, half(h)])
                fed = (S_hi[:, h], S_lo[:, h])
                prior = not (first and k == 0)
                if prior:
                    pe.wait_ge(r_act, HS * p + k)
                product(p_r, (wh_hi, wh_lo), l, 0, state, True, False)
                if prior:
                    pe.wait_ge(z_act, HS * p + k)
                product(p_z, (wh_hi, wh_lo), l, 1, state, True, False)
                if prior:
                    pe.wait_ge(t_mul, HS * p + k)
                product(p_hn, (wh_hi, wh_lo), l, 2, state, True, True).then_inc(hn_done, 1)
                pe.wait_ge(s_split, HS * p + k + 1)
                product(p_r, (wx_hi, wx_lo), l, 0, fed, False, True).then_inc(r_done, 1)
                if prior:
                    pe.wait_ge(t_add, HS * p + k)
                product(p_xn, (wx_hi, wx_lo), l, 2, fed, True, True).then_inc(xn_done, 1)
                product(p_z, (wx_hi, wx_lo), l, 1, fed, False, True).then_inc(z_done, 1)

            def transpose_former(p, g, h, first):
                if g == 0:
                    if not first:
                        pe.wait_ge(xT_done, 4 * p + h + 1)
                        transpose_h(p - 1, STEPS - 1, h)
                else:
                    if g == 1:
                        pe.wait_ge(xT_done, 4 * p + 2 + h + 1)
                    else:
                        pe.wait_ge(nat_split, HS_IN * p + 2 * (g - 2) + h + 1)
                    transpose_h(p, g - 1, h)

            def body(p, first, last):
                for g in range(STEPS):
                    if g < 2 and not (first and g == 0):
                        transpose_x(p, g, first)
                    aggregate(p, g, first)
                    if g == 0 and first:
                        pe.wait_ge(start_lo, L)
                        pe.wait_ge(rows_out, 2)
                    for h in range(2):
                        transpose_former(p, g, h, first)
                        gates(p, g, h, first)

            pairs(pe, body)
            pe.wait_ge(low_red, 1)
            pe.wait_ge(r_act, HS * PAIRS)
            nc.tensor.matmul(p_r[0:1, 0:1], lowf[:, 0:1], ones[:, 0:1], start=True, stop=True).then_inc(low_sum, 1)
            for h in range(2):
                pe.wait_ge(y_added, 4 * (PAIRS - 1) + h + 1)
                transpose_h(PAIRS - 1, STEPS - 1, h)

            def graph(b):
                pe.wait_ge(g_loaded, 48 * b + 48)
                for h in range(2):
                    for i in range(HB):
                        last = nc.tensor.transpose(p_tr[h][:, i, :], x_in[:, 0, h * HB + i], ident[:, :])
                    last.then_inc(g_xtr, 1)
                for l in range(L):
                    if l:
                        pe.wait_ge(g_nat, (L - 1) * b + l)
                    for h in range(2):
                        for j in range(NB):
                            last = nc.tensor.matmul(p_S[h][:, :], x_in[:, 0, j], adj_in[:, j, half(h)],
                                                    start=(j == 0), stop=(j == NB - 1))
                        last.then_inc(g_s, 1)
                    for h in range(2):
                        m = 2 * L * b + 2 * l + h
                        if l == 0:
                            pe.wait_ge(g_xT, 2 * b + h + 1)
                        if l or h:
                            pe.wait_ge(g_dve, CHAIN * m)
                        pe.wait_ge(g_s_out, m + 1)
                        for bank, q, fed, state in ((p_r, 0, True, True), (p_z, 1, True, True),
                                                    (p_hn, 2, False, True), (p_xn, 2, True, False)):
                            terms = []
                            if fed:
                                terms += [(w, g_S[:, half(h)]) for w in (wx_hi, wx_lo)]
                            if state:
                                terms += [(w, hT[:, 0, half(h)]) for w in (wh_hi, wh_lo)]
                            for n, (w, v) in enumerate(terms):
                                last = nc.tensor.matmul(bank[:, :], w[:, l, q * C:(q + 1) * C].bitcast(F32), v,
                                                        start=(n == 0), stop=(n == len(terms) - 1))
                        last.then_inc(g_gates, 1)
                    pe.wait_ge(g_dve, CHAIN * (2 * L * b + 2 * l + 2))
                    for j in range(NB):
                        last = nc.tensor.transpose(p_tr[j // HB][:, j % HB, :], hT[:, 0, j * P:(j + 1) * P], ident[:, :])
                    last.then_inc(g_tr, 1)

            general(pe, graph)

        @block.scalar
        def _(act):
            def copy(dst, src):
                return nc.scalar.activation(dst, src, ACT.Copy)

            act.wait_ge(ones_made, 1)
            nc.scalar.activation(act_scratch[:, :], ones[:, :], ACT.Sigmoid)

            def split_w_hh(l):
                act.wait_ge(start_tr, l + 1)
                if l == L - 1:
                    act.wait_ge(rows_out, 1)
                copy(wh_hi[:, l], p_start[l][1][:, 0:G * C])

            def split_joined(l):
                act.wait_ge(start_joined, l + 1)
                copy(wx_hi[:, l], p_start[l][0][:, 0:G * C]).then_inc(start_hi, 1)

            def take_adj(p, s, j, first=False):
                act.wait_ge(adj_loaded[j], 16 * (2 * p + s + 1))
                copy(adj_hi[:, s, j], adj_in[:, j]).then_inc(adj_ready, 2 if first and s == 1 else 1)

            def split_x(p, s, first):
                act.wait_ge(x_loaded[s], 16 * (p + 1))
                if not first:
                    act.wait_ge(s_done, HS * (p - 1) + 2 * (STEPS - 2 + s) + 2)
                copy(nat_hi[:, s], x_in[:, s]).then_inc(xnat_hi, 1)

            def take_xT(p, s):
                for h in range(2):
                    act.wait_ge(x_tr, 4 * p + 2 * s + h + 1)
                    copy(hT_hi[:, s, half(h)], flat(p_tr[h])).then_inc(xT_hi, 1)

            def take_former(p, g, h):
                act.wait_ge(h_tr, HS * p + 2 * g + h + 1)
                copy(nat_hi[:, g % 2, h * HB:(h + 1) * HB], p_tr[h][:, :, :]).then_inc(nat_hi_made, 1)

            def gate(dst, bank, done, made, func, b, p, k):
                act.wait_ge(done, HS * p + k + 1)
                nc.scalar.activation(dst, bank, func, bias=b).then_inc(made, 1)

            def s_high(p, g, h):
                act.wait_ge(s_done, HS * p + 2 * g + h + 1)
                copy(S_hi[:, h], p_S[h][:, :]).then_inc(s_hi_made, 1)

            def h_high(p, g, h):
                act.wait_ge(h_new, HS * p + 2 * g + h + 1)
                copy(hT_hi[:, g % 2, half(h)], hT[:, g % 2, half(h)]).then_inc(h_hi_made, 1)

            def body(p, first, last):
                for g in range(STEPS):
                    l, s = divmod(g, 2)
                    places = ((),) * 4
                    if g == 0:
                        graph_of = (p, 1)
                        places = ((), (0,), (2, 4), (6,)) if first else ((), (4, 5), (6, 7), ())
                    elif g == STEPS - 2 and not last:
                        graph_of = (p + 1, 0)
                        places = ((), (0,), (1,), (2, 3, 4, 5))
                    elif g == STEPS - 1 and not last:
                        graph_of = (p + 1, 0)
                        places = ((6,), (7,), (), ())

                    def fill(n):
                        for j in places[n]:
                            take_adj(*graph_of, j, first and g == 0)

                    if l == 0 and not (first and g == 0):
                        take_xT(p, s)
                    s_high(p, g, 0)
                    if 1 <= g <= STEPS - 2:
                        h_high(p, g - 1, 1)
                    if g == 0:
                        split_x(p, 1, first)
                    elif g == STEPS - 1 and not last:
                        split_x(p + 1, 0, False)
                    fill(0)
                    s_high(p, g, 1)
                    if 1 <= g <= STEPS - 2:
                        take_former(p, g - 1, 0)
                    fill(1)
                    for h in range(2):
                        k = 2 * g + h
                        gate(r_sb[:, h], p_r[:, :], r_done, r_act, ACT.Sigmoid, bsum[:, G * l:G * l + 1], p, k)
                        gate(z_sb[:, h], p_z[:, :], z_done, z_act, ACT.Sigmoid, bsum[:, G * l + 1:G * l + 2], p, k)
                        if h == 0 and 1 <= g <= STEPS - 2:
                            take_former(p, g - 1, 1)
                        gate(n_sb[:, h], t_sb[:, h], t_add, n_act, ACT.Tanh, bias[:, 0, G * l + 2:G * l + 3], p, k)
                        if h == 0:
                            fill(2)
                            if g == STEPS - 1 and not last:
                                take_adj(p + 1, 1, 0)
                    if l < L - 1:
                        h_high(p, g, 0)
                    fill(3)
                    if g == STEPS - 1 and not last:
                        for j in range(1, 4):
                            take_adj(p + 1, 1, j)

            split_w_hh(0)
            split_w_hh(1)
            split_joined(0)
            split_w_hh(2)
            split_joined(1)
            split_x(0, 0, True)
            split_joined(2)
            split_w_hh(3)
            take_adj(0, 0, 0)
            split_joined(3)
            for j in range(1, NB):
                if j == NB - 2:
                    take_xT(0, 0)
                take_adj(0, 0, j)
            act.wait_ge(rows_out, 2)
            pairs(act, body)
            act.wait_ge(shift_made, 1)
            for j in range(NB):
                last = nc.scalar.activation(y[:, 0, j], y[:, 0, j], ACT.Identity, bias=shift[:, j:j + 1],
                                            scale=rstd[:, 0, j:j + 1])
            last.then_inc(y0_normed, 1)

            def graph(b):
                for h in range(2):
                    act.wait_ge(g_xtr, 2 * b + h + 1)
                    copy(hT[:, 0, half(h)], flat(p_tr[h])).then_inc(g_xT, 1)
                for l in range(L):
                    for h in range(2):
                        act.wait_ge(g_s, 2 * L * b + 2 * l + h + 1)
                        copy(g_S[:, half(h)], p_S[h][:, :]).then_inc(g_s_out, 1)
                    for h in range(2):
                        m = 2 * L * b + 2 * l + h
                        act.wait_ge(g_gates, m + 1)
                        nc.scalar.activation(r_sb[:, 0], p_r[:, :], ACT.Sigmoid, bias=bsum[:, G * l:G * l + 1])
                        nc.scalar.activation(z_sb[:, 0], p_z[:, :], ACT.Sigmoid,
                                             bias=bsum[:, G * l + 1:G * l + 2]).then_inc(g_rz, 1)
                        act.wait_ge(g_dve, CHAIN * m + 2)
                        nc.scalar.activation(n_sb[:, 0], t_sb[:, 0], ACT.Tanh,
                                             bias=bias[:, 0, G * l + 2:G * l + 3]).then_inc(g_n, 1)

            general(act, graph)

        @block.vector
        def _(dve):
            def lo(dst, src, hi):
                return nc.vector.tensor_tensor(dst, src, hi.bitcast(F32), ALU.subtract)

            nc.vector.memset(ones[:, :], 1.0).then_inc(ones_made, 1)
            nc.vector.memset(low[:, :], 0).then_inc(low_zero, 1)
            dve.wait_ge(low_zero, 1)

            def copy_weights(l):
                dve.wait_ge(start_tr, l + 1)
                nc.vector.tensor_copy(w_tr[:, l], p_start[l][0][:, 0:(1 + G) * C]).then_inc(start_copied, 1)

            def split_weights(l):
                dve.wait_ge(start_hi, l + 1)
                lo(wh_lo[:, l], p_start[l][1][:, 0:G * C], wh_hi[:, l])
                lo(wx_lo[:, l], p_start[l][0][:, 0:G * C], wx_hi[:, l]).then_inc(start_lo, 1)

            def split_x(p, s):
                dve.wait_ge(xnat_hi, 2 * p + s + 1)
                lo(nat_lo[:, s], x_in[:, s], nat_hi[:, s]).then_inc(xnat_lo, 1)

            for l in range(L - 1):
                copy_weights(l)
            split_weights(0)
            split_weights(1)
            copy_weights(3)
            nc.vector.tensor_copy(bias[:, :, :].rearrange("p a b -> p (a b)"), p_rows[:, 0:2 * L * G])
            nc.vector.tensor_copy(mask[:, :], p_rows[:, 2 * L * G:2 * L * G + B * NB]).then_inc(rows_out, 1)
            split_x(0, 0)
            split_weights(2)
            split_weights(3)
            dve.wait_ge(rows_out, 1)
            nc.vector.tensor_tensor(bsum[:, :], bias[:, 0], bias[:, 1], ALU.add).then_inc(rows_out, 1)

            def check_adj(p, s, j, first=False):
                dve.wait_ge(adj_loaded[j], 16 * (2 * p + s + 1))
                if not (first and s == 0 and j == 0):
                    dve.wait_ge(adj_checked, NB * (2 * p + s) + j)
                nc.vector.tensor_tensor(low[:, :], low[:, :], adj_in[:, j].bitcast(I32),
                                        ALU.bitwise_or).then_inc(adj_checked, 1)

            def take_xT(p, s):
                for h in range(2):
                    dve.wait_ge(xT_hi, 4 * p + 2 * s + h + 1)
                    lo(hT_lo[:, s, half(h)], flat(p_tr[h]), hT_hi[:, s, half(h)]).then_inc(xT_done, 1)

            def take_adj1(j):
                dve.wait_ge(adj_loaded[j], 32)
                nc.vector.tensor_copy(adj_hi[:, 1, j], adj_in[:, j]).then_inc(adj1_ready, 1)

            def take_former(p, g, h):
                dve.wait_ge(nat_hi_made, HS_IN * p + 2 * g + h + 1)
                lo(nat_lo[:, g % 2, h * HB:(h + 1) * HB], p_tr[h][:, :, :],
                   nat_hi[:, g % 2, h * HB:(h + 1) * HB]).then_inc(nat_split, 1)

            def residual(p, s, h, measured=True):
                if h == 0:
                    dve.wait_ge(y_loaded[s], 16 * (p + 1))
                dve.wait_ge(h_tr, HS * p + 2 * (STEPS - 2 + s) + h + 1)
                for i in range(HB):
                    j = h * HB + i
                    col = NB * (2 * p + s) + j
                    last = nc.vector.scalar_tensor_tensor(y[:, s, j], p_tr[h][:, i, :], mask[:, bass.ds(col, 1)],
                                                          y[:, s, j], ALU.mult, ALU.add)
                last.then_inc(y_added, 1)
                if measured:
                    measure(p, s, h)

            def measure(p, s, h):
                dve.wait_ge(y_added, 4 * p + 2 * s + h + 1)
                for i in range(HB):
                    j = h * HB + i
                    last = nc.vector.bn_stats(stats[:, j], y[:, s, j])
                last.then_inc(y_stats, 1)

            def wait_stats(p, s, h):
                dve.wait_ge(y_stats, 4 * p + 2 * s + h + 1)

            def moments(s, h):
                for j in range(h * HB, (h + 1) * HB):
                    last = nc.vector.bn_aggr(mv[:, s, j], stats[:, j])
                if h == 1:
                    last.then_inc(y_aggr, 1)

            def variance_eps(p, s):
                dve.wait_ge(y_aggr, 2 * p + s + 1)
                nc.vector.tensor_scalar(vare[:, s], mv[:, s, :, 1], EPS, None, ALU.add).then_inc(var_eps, 1)

            def normalise(p, s):
                dve.wait_ge(rstd_made, 2 * p + s + 1)
                for j in range(NB):
                    last = nc.vector.tensor_scalar(y[:, s, j], y[:, s, j], mv[:, s, j, 0:1], rstd[:, s, j:j + 1],
                                                   ALU.subtract, ALU.mult)
                last.then_inc(y_normed, 1)

            def s_low(p, g, h):
                dve.wait_ge(s_hi_made, HS * p + 2 * g + h + 1)
                lo(S_lo[:, h], p_S[h][:, :], S_hi[:, h]).then_inc(s_split, 1)

            def update(p, g, h):
                dve.wait_ge(n_act, HS * p + 2 * g + h + 1)
                nc.vector.tensor_tensor(t_sb[:, h], hT[:, g % 2, half(h)], n_sb[:, h], ALU.subtract).then_inc(d_sub, 1)
                dve.wait_ge(d_sub, HS * p + 2 * g + h + 1)
                nc.vector.tensor_tensor(t_sb[:, h], z_sb[:, h], t_sb[:, h], ALU.mult).then_inc(d_mul, 1)

            def new_state(p, g, h):
                dve.wait_ge(d_mul, HS * p + 2 * g + h + 1)
                nc.vector.tensor_tensor(hT[:, g % 2, half(h)], n_sb[:, h], t_sb[:, h], ALU.add).then_inc(h_new, 1)

            def h_low(p, g, h):
                dve.wait_ge(h_hi_made, HS_IN * p + 2 * g + h + 1)
                lo(hT_lo[:, g % 2, half(h)], hT[:, g % 2, half(h)], hT_hi[:, g % 2, half(h)]).then_inc(h_split, 1)

            def mask_low():
                dve.wait_ge(adj_checked, B * NB)
                nc.vector.tensor_scalar(low[:, :], low[:, :], LOWBITS, None, ALU.bitwise_and).then_inc(low_masked, 1)
                dve.wait_ge(low_masked, 1)
                nc.vector.tensor_reduce(lowf[:, :], low[:, :], AX.X, ALU.max).then_inc(low_red, 1)

            def body(p, first, last):
                checks = [(p, 1, j) for j in range(NB)] + [(p + 1, 0, j) for j in range(NB) if not last]
                if first:
                    checks = [(0, 0, NB - 2), (0, 0, NB - 1)] + checks

                def fill(g):
                    if checks and (g or (first and checks[0][1] == 0)):
                        check_adj(*checks.pop(0))

                for g in range(STEPS):
                    l, s = divmod(g, 2)
                    ended = (p, 0) if g == STEPS - 1 else (p - 1, 1) if g == 0 and not first else None
                    if g:
                        new_state(p, g - 1, 1)
                        if first and g == 1:
                            take_adj1(7)
                    elif not first:
                        new_state(p - 1, STEPS - 1, 1)
                    if l == 0 and not (first and g == 0):
                        take_xT(p, s)
                    s_low(p, g, 0)
                    if 1 <= g <= STEPS - 2:
                        h_low(p, g - 1, 1)
                    if g == 0:
                        split_x(p, 1)
                    elif g == STEPS - 1 and not last:
                        split_x(p + 1, 0)
                    fill(g)
                    s_low(p, g, 1)
                    for h in range(2):
                        k = 2 * g + h
                        if h == 0:
                            if ended:
                                residual(*ended, 0)
                                wait_stats(*ended, 0)
                            elif g:
                                take_former(p, g - 1, 0)
                        dve.wait_ge(hn_done, HS * p + k + 1)
                        dve.wait_ge(r_act, HS * p + k + 1)
                        nc.vector.scalar_tensor_tensor(t_sb[:, h], p_hn[:, :], bias[:, 1, G * l + 2:G * l + 3],
                                                       r_sb[:, h], ALU.add, ALU.mult).then_inc(t_mul, 1)
                        if ended and not (last and g == STEPS - 1 and h == 1):
                            moments(ended[1], h)
                        dve.wait_ge(xn_done, HS * p + k + 1)
                        dve.wait_ge(t_mul, HS * p + k + 1)
                        nc.vector.tensor_tensor(t_sb[:, h], p_xn[:, :], t_sb[:, h], ALU.add).then_inc(t_add, 1)
                        if last and g == STEPS - 1:
                            if h == 0:
                                residual(*ended, 1, False)
                            else:
                                measure(*ended, 1)
                            update(p, g, h)
                            new_state(p, g, h)
                            if h == 1:
                                wait_stats(*ended, 1)
                                moments(ended[1], 1)
                        elif h == 0:
                            if ended:
                                residual(*ended, 1)
                                wait_stats(*ended, 1)
                            elif g:
                                take_former(p, g - 1, 1)
                            fill(g)
                            if first and g == 0:
                                take_adj1(1)
                    if first and g == 0:
                        take_adj1(3)
                    if ended:
                        variance_eps(*ended)
                    if last and g == STEPS - 1:
                        break
                    new_state(p, g, 0)
                    if l < L - 1:
                        h_low(p, g, 0)
                    if first and g == 0:
                        take_adj1(5)
                    if 1 <= g <= 2 and not first:
                        normalise(p - 1, g - 1)
                    fill(g)
                    if last and g == STEPS // 2:
                        mask_low()

            for j in range(NB - 2):
                check_adj(0, 0, j, True)
            take_xT(0, 0)
            pairs(dve, body)
            def last_normalise(h):
                dve.wait_ge(rstd_made, B + h)
                for j in range(h * HB, (h + 1) * HB):
                    last = nc.vector.tensor_scalar(y[:, 1, j], y[:, 1, j], mv[:, 1, j, 0:1], rstd[:, 1, j:j + 1],
                                                   ALU.subtract, ALU.mult)
                last.then_inc(y_normed, 1)

            for h in range(2):
                residual(PAIRS - 1, 1, h)
                if h == 0:
                    dve.wait_ge(rstd_made, B - 1)
                    nc.vector.scalar_tensor_tensor(shift[:, :], mv[:, 0, :, 0], -1.0, rstd[:, 0], ALU.mult,
                                                   ALU.mult).then_inc(shift_made, 1)
                wait_stats(PAIRS - 1, 1, h)
                for j in range(h * HB, (h + 1) * HB):
                    last = nc.vector.bn_aggr(mv[:, 1, j], stats[:, j])
                last.then_inc(y_aggr, 1)
                dve.wait_ge(y_aggr, B + h)
                nc.vector.tensor_scalar(vare[:, 1, h * HB:(h + 1) * HB], mv[:, 1, h * HB:(h + 1) * HB, 1], EPS, None,
                                        ALU.add).then_inc(var_eps, 1)
            dve.wait_ge(low_sum, 1)
            nc.vector.tensor_scalar(flag[0:1, :], p_r[0:1, 0:1], 0.0, None, ALU.is_gt).then_inc(flag_made, 1)
            for h in range(2):
                last_normalise(h)

            def graph(b):
                for l in range(L):
                    for h in range(2):
                        m = 2 * L * b + 2 * l + h
                        n, t, z = n_sb[:, 0], t_sb[:, 0], z_sb[:, 0]
                        dve.wait_ge(g_rz, m + 1)
                        nc.vector.scalar_tensor_tensor(t, p_hn[:, :], bias[:, 1, G * l + 2:G * l + 3],
                                                       r_sb[:, 0], ALU.add, ALU.mult).then_inc(g_dve, 1)
                        dve.wait_ge(g_dve, CHAIN * m + 1)
                        nc.vector.tensor_tensor(t, p_xn[:, :], t, ALU.add).then_inc(g_dve, 1)
                        dve.wait_ge(g_n, m + 1)
                        nc.vector.tensor_tensor(t, hT[:, 0, half(h)], n, ALU.subtract).then_inc(g_dve, 1)
                        dve.wait_ge(g_dve, CHAIN * m + 3)
                        nc.vector.tensor_tensor(t, z, t, ALU.mult).then_inc(g_dve, 1)
                        dve.wait_ge(g_dve, CHAIN * m + 4)
                        nc.vector.tensor_tensor(hT[:, 0, half(h)], n, t, ALU.add).then_inc(g_dve, 1)
                    dve.wait_ge(g_tr, L * b + l + 1)
                    for h in range(2):
                        if l < L - 1:
                            last = nc.vector.tensor_copy(x_in[:, 0, h * HB:(h + 1) * HB], p_tr[h][:, :, :])
                        if l == L - 1:
                            for i in range(HB):
                                j = h * HB + i
                                last = nc.vector.scalar_tensor_tensor(
                                    y[:, 0, j], p_tr[h][:, i, :], mask[:, bass.ds(NB * b + j, 1)], y[:, 0, j],
                                    ALU.mult, ALU.add)
                    last.then_inc(g_nat if l < L - 1 else g_added, 1)
                dve.wait_ge(g_added, b + 1)
                for j in range(NB):
                    last = nc.vector.bn_stats(stats[:, j], y[:, 0, j])
                last.then_inc(g_stats, 1)
                dve.wait_ge(ident_made, 1)
                dve.wait_ge(g_stats, b + 1)
                for j in range(NB):
                    last = nc.vector.bn_aggr(mv[:, 0, j], stats[:, j])
                last.then_inc(g_aggr, 1)
                dve.wait_ge(g_aggr, b + 1)
                nc.vector.tensor_scalar(vare[:, 0], mv[:, 0, :, 1], EPS, None, ALU.add).then_inc(g_var, 1)
                dve.wait_ge(g_rstd, b + 1)
                for j in range(NB):
                    last = nc.vector.tensor_scalar(y[:, 0, j], y[:, 0, j], mv[:, 0, j, 0:1], rstd[:, 0, j:j + 1],
                                                   ALU.subtract, ALU.mult)
                last.then_inc(g_normed, 1)

            general(dve, graph)

        @block.gpsimd
        def _(pool):
            nc.gpsimd.memset(ident[:, :], 0.0).then_inc(ident_zero, 1)
            pool.wait_ge(ident_zero, 1)
            nc.gpsimd.affine_select(out=ident[:, :], in_=ident[:, :], compare_op=ALU.not_equal, fill=1.0,
                                    base=0, pattern=[[-1, P]], channel_multiplier=1).then_inc(ident_made, 1)
            nc.gpsimd.memset(mhalf[:, :], -0.5)

            def inverse_deviation(p, s):
                pool.wait_ge(var_eps, 2 * p + s + 1)
                nc.gpsimd.tensor_tensor(rstd[:, s], vare[:, s], mhalf[:, :], ALU.pow).then_inc(rstd_made, 1)

            def body(p, first, last):
                for g in range(STEPS):
                    l, s = divmod(g, 2)
                    if l == 0:
                        for h in range(2):
                            pool.wait_ge(xT_done, 4 * p + 2 * s + h + 1)
                            nc.gpsimd.tensor_tensor(hT[:, s, half(h)], hT_hi[:, s, half(h)].bitcast(F32),
                                                    hT_lo[:, s, half(h)].bitcast(F32), ALU.add).then_inc(xT_whole, 1)
                    for h in range(0 if last and g == STEPS - 1 else 2):
                        k = 2 * g + h
                        if l == 0:
                            pool.wait_ge(xT_whole, 4 * p + k + 1)
                        pool.wait_ge(n_act, HS * p + k + 1)
                        nc.gpsimd.tensor_tensor(t_sb[:, h], hT[:, s, half(h)], n_sb[:, h],
                                                ALU.subtract).then_inc(d_sub, 1)
                        pool.wait_ge(d_sub, HS * p + k + 1)
                        nc.gpsimd.tensor_tensor(t_sb[:, h], z_sb[:, h], t_sb[:, h],
                                                ALU.mult).then_inc(d_mul, 1)
                    if g == 0 and not first:
                        inverse_deviation(p - 1, 1)
                    elif g == STEPS - 1:
                        inverse_deviation(p, 0)

            pairs(pool, body)
            for h in range(2):
                pool.wait_ge(var_eps, B + h)
                nc.gpsimd.tensor_tensor(rstd[:, 1, h * HB:(h + 1) * HB], vare[:, 1, h * HB:(h + 1) * HB],
                                        mhalf[:, 0:HB], ALU.pow).then_inc(rstd_made, 1)

            def graph(b):
                pool.wait_ge(g_var, b + 1)
                nc.gpsimd.tensor_tensor(rstd[:, 0], vare[:, 0], mhalf[:, :], ALU.pow).then_inc(g_rstd, 1)

            general(pool, graph)


_INS = ['x', 'adj', 'nodemask', 'L0_gnn_weight', 'L0_gnn_w_ih', 'L0_gnn_w_hh', 'L0_gnn_b_ih', 'L0_gnn_b_hh']


def kernel(**inputs):
    import numpy as _np
    import concourse.bacc as _bacc
    from concourse import mybir as _mybir
    from concourse.bass_utils import run_bass_kernel_spmd as _run

    nc = _bacc.Bacc("TRN2", target_bir_lowering=False, num_devices=1)
    arrays, args = {}, []
    for name in _INS:
        a = _np.ascontiguousarray(inputs[name])
        arrays[f"in_{name}_dram"] = a
        args.append(nc.dram_tensor(f"in_{name}_dram", a.shape, _mybir.dt.from_np(a.dtype), kind="ExternalInput").ap())
    out = nc.dram_tensor("out_0_dram", inputs["x"].shape, _mybir.dt.float32, kind="ExternalOutput").ap()
    gnn_kernel(nc, *args, out)
    r = _run(nc, [arrays], core_ids=[0])
    return r.results[0]["out_0_dram"]
```
